# Optimizing a Trainium2 kernel written in Bass

```python
import numpy as np
import jax
import jax.numpy as jnp

def _softmax(x, axis=-1):
    return jax.nn.softmax(x, axis=axis)

def _gelu(x):
    return jax.nn.gelu(x, approximate=True)

def _silu(x):
    return jax.nn.silu(x)

def _sigmoid(x):
    return jax.nn.sigmoid(x)

def _layernorm(x, axis=-1, eps=1e-05):
    m = jnp.mean(x, axis=axis, keepdims=True)
    v = jnp.var(x, axis=axis, keepdims=True)
    return (x - m) / jnp.sqrt(v + eps)

def _scatter_add(tgt, idx, src, axis=0):
    return tgt.at[idx].add(src)

def _segment_sum(src, seg, n):
    return jax.ops.segment_sum(src, seg, n)
kernel_name = 'mk_lm_tower_d2_tok_ids1024_r4_7d6517'

def setup_inputs(seed: int=0):
    np.random.seed(seed)
    _w = jnp.asarray

    def _rec_inputs():
        import jax
        import jax.numpy as jnp
        _rk = jax.random.key(seed)
        x = jax.random.randint(jax.random.fold_in(_rk, 1), (2, 1024), 0, 12564, jnp.int32)
        return x
    x = _rec_inputs()

    def _L0_tok_setup():
        import jax, jax.numpy as jnp
        import numpy as np
        VOCAB = 50257
        D_MODEL = 256
        BATCH = 4
        SEQ = 1024
        key = jax.random.key(seed)
        k_x, k_w = jax.random.split(key)
        x = jax.random.randint(k_x, (BATCH, SEQ), 0, VOCAB, dtype=jnp.int64 if jax.config.jax_enable_x64 else jnp.int32)
        W = jax.random.truncated_normal(k_w, -3.0, 3.0, (VOCAB, D_MODEL), dtype=jnp.float32)
        return {'x': x, 'W': W}
    _L0_tok_all = _L0_tok_setup()
    _L0_tok_in = {k: v for k, v in _L0_tok_all.items() if k in ('W',)}
    del _L0_tok_all

    def _L0_attn_setup():
        import jax, jax.numpy as jnp
        import numpy as np
        B, N, C = (2, 512, 256)
        H = 16
        D = C // H
        key = jax.random.key(seed)
        ks = jax.random.split(key, 5)
        s = 0.02
        return {'x': jax.random.normal(ks[0], (B, N, C), dtype=jnp.float32), 'qkv_w': jax.random.normal(ks[1], (C, 3 * C), dtype=jnp.float32) * s, 'qkv_b': jax.random.normal(ks[2], (3 * C,), dtype=jnp.float32) * s, 'proj_w': jax.random.normal(ks[3], (C, C), dtype=jnp.float32) * s, 'proj_b': jax.random.normal(ks[4], (C,), dtype=jnp.float32) * s}
    _L0_attn_all = _L0_attn_setup()
    _L0_attn_in = {k: v for k, v in _L0_attn_all.items() if k in ('qkv_w', 'qkv_b', 'proj_w', 'proj_b')}
    del _L0_attn_all

    def _L0_ffn_setup():
        import jax, jax.numpy as jnp
        import numpy as np
        B, S, D = (4, 512, 256)
        N_EXPERTS, EXPERT_SIZE = (16, 64)
        WIDTH = N_EXPERTS * EXPERT_SIZE
        key = jax.random.key(seed)
        k_x, k_w1, k_w2, k_g = jax.random.split(key, 4)
        x = jax.random.normal(k_x, (B, S, D), dtype=jnp.float32)
        w1 = jax.random.normal(k_w1, (D, WIDTH), dtype=jnp.float32) / np.sqrt(D).astype(np.float32)
        b1 = jnp.zeros((WIDTH,), dtype=jnp.float32)
        w2 = jax.random.normal(k_w2, (WIDTH, D), dtype=jnp.float32) / np.sqrt(WIDTH).astype(np.float32)
        b2 = jnp.zeros((D,), dtype=jnp.float32)
        return {'x': x, 'w1': w1, 'b1': b1, 'w2': w2, 'b2': b2}
    _L0_ffn_all = _L0_ffn_setup()
    _L0_ffn_in = {k: v for k, v in _L0_ffn_all.items() if k in ('w1', 'b1', 'w2', 'b2')}
    del _L0_ffn_all

    def _L1_attn_setup():
        import jax, jax.numpy as jnp
        import numpy as np
        HIDDEN = 256
        B, S = (8, 512)
        key = jax.random.key(seed)
        k1, k2, k3, k4 = jax.random.split(key, 4)
        gain = 1.2
        bound = gain * np.sqrt(6.0 / (HIDDEN + HIDDEN))
        return {'hidden_states': jax.random.normal(k1, (B, S, HIDDEN), dtype=jnp.float32), 'Wq': jax.random.uniform(k2, (HIDDEN, HIDDEN), jnp.float32, -bound, bound), 'bq': jnp.zeros((HIDDEN,), jnp.float32), 'Wv': jax.random.uniform(k3, (HIDDEN, HIDDEN), jnp.float32, -bound, bound), 'bv': jnp.zeros((HIDDEN,), jnp.float32), 'anomaly_matrix': jax.random.uniform(k4, (HIDDEN, HIDDEN), jnp.float32, -2.0, 2.0)}
    _L1_attn_all = _L1_attn_setup()
    _L1_attn_in = {k: v for k, v in _L1_attn_all.items() if k in ('Wq', 'bq', 'Wv', 'bv', 'anomaly_matrix')}
    del _L1_attn_all

    def _L1_ffn_setup():
        import jax, jax.numpy as jnp
        import numpy as np
        D_MODEL = 256
        HIDDEN = 512
        MOE_DIM = 64
        N_EXPERTS = 8
        TOP_K = 2
        EXP_HIDDEN = HIDDEN // 2
        B, S = (4, 512)
        key = jax.random.key(seed)
        ks = jax.random.split(key, 20)

        def w(k, shape, fan_in):
            return (jax.random.normal(k, shape, dtype=jnp.float32) / np.sqrt(fan_in)).astype(jnp.float32)
        return {'inputs_embeds': jax.random.normal(ks[0], (B, S, D_MODEL), dtype=jnp.float32), 'enc_w': w(ks[1], (D_MODEL, HIDDEN), D_MODEL), 'enc_b': jnp.zeros((HIDDEN,), jnp.float32), 's2c_w': w(ks[2], (HIDDEN, MOE_DIM), HIDDEN), 's2c_b': jnp.zeros((MOE_DIM,), jnp.float32), 'r_w1': w(ks[3], (MOE_DIM, 64), MOE_DIM), 'r_b1': jnp.zeros((64,), jnp.float32), 'r_w2': w(ks[4], (64, N_EXPERTS), 64), 'r_b2': jnp.zeros((N_EXPERTS,), jnp.float32), 'e_w1': w(ks[5], (N_EXPERTS, MOE_DIM, EXP_HIDDEN), MOE_DIM), 'e_b1': jnp.zeros((N_EXPERTS, EXP_HIDDEN), jnp.float32), 'e_w2': w(ks[6], (N_EXPERTS, EXP_HIDDEN, MOE_DIM), EXP_HIDDEN), 'e_b2': jnp.zeros((N_EXPERTS, MOE_DIM), jnp.float32), 'c2s_w': w(ks[7], (MOE_DIM, HIDDEN), MOE_DIM), 'c2s_b': jnp.zeros((HIDDEN,), jnp.float32), 'dec_w': w(ks[8], (HIDDEN, D_MODEL), HIDDEN), 'dec_b': jnp.zeros((D_MODEL,), jnp.float32), 'ln_g': jnp.ones((D_MODEL,), jnp.float32), 'ln_b': jnp.zeros((D_MODEL,), jnp.float32)}
    _L1_ffn_all = _L1_ffn_setup()
    _L1_ffn_in = {k: v for k, v in _L1_ffn_all.items() if k in ('enc_w', 'enc_b', 's2c_w', 's2c_b', 'r_w1', 'r_b1', 'r_w2', 'r_b2', 'e_w1', 'e_b1', 'e_w2', 'e_b2', 'c2s_w', 'c2s_b', 'dec_w', 'dec_b', 'ln_g', 'ln_b')}
    del _L1_ffn_all
    return {'x': x, 'L0_tok_W': _L0_tok_in['W'], 'L0_attn_qkv_w': _L0_attn_in['qkv_w'], 'L0_attn_qkv_b': _L0_attn_in['qkv_b'], 'L0_attn_proj_w': _L0_attn_in['proj_w'], 'L0_attn_proj_b': _L0_attn_in['proj_b'], 'L0_ffn_w1': _L0_ffn_in['w1'], 'L0_ffn_b1': _L0_ffn_in['b1'], 'L0_ffn_w2': _L0_ffn_in['w2'], 'L0_ffn_b2': _L0_ffn_in['b2'], 'L1_attn_Wq': _L1_attn_in['Wq'], 'L1_attn_bq': _L1_attn_in['bq'], 'L1_attn_Wv': _L1_attn_in['Wv'], 'L1_attn_bv': _L1_attn_in['bv'], 'L1_attn_anomaly_matrix': _L1_attn_in['anomaly_matrix'], 'L1_ffn_enc_w': _L1_ffn_in['enc_w'], 'L1_ffn_enc_b': _L1_ffn_in['enc_b'], 'L1_ffn_s2c_w': _L1_ffn_in['s2c_w'], 'L1_ffn_s2c_b': _L1_ffn_in['s2c_b'], 'L1_ffn_r_w1': _L1_ffn_in['r_w1'], 'L1_ffn_r_b1': _L1_ffn_in['r_b1'], 'L1_ffn_r_w2': _L1_ffn_in['r_w2'], 'L1_ffn_r_b2': _L1_ffn_in['r_b2'], 'L1_ffn_e_w1': _L1_ffn_in['e_w1'], 'L1_ffn_e_b1': _L1_ffn_in['e_b1'], 'L1_ffn_e_w2': _L1_ffn_in['e_w2'], 'L1_ffn_e_b2': _L1_ffn_in['e_b2'], 'L1_ffn_c2s_w': _L1_ffn_in['c2s_w'], 'L1_ffn_c2s_b': _L1_ffn_in['c2s_b'], 'L1_ffn_dec_w': _L1_ffn_in['dec_w'], 'L1_ffn_dec_b': _L1_ffn_in['dec_b'], 'L1_ffn_ln_g': _L1_ffn_in['ln_g'], 'L1_ffn_ln_b': _L1_ffn_in['ln_b']}

def reference(x, L0_tok_W, L0_attn_qkv_w, L0_attn_qkv_b, L0_attn_proj_w, L0_attn_proj_b, L0_ffn_w1, L0_ffn_b1, L0_ffn_w2, L0_ffn_b2, L1_attn_Wq, L1_attn_bq, L1_attn_Wv, L1_attn_bv, L1_attn_anomaly_matrix, L1_ffn_enc_w, L1_ffn_enc_b, L1_ffn_s2c_w, L1_ffn_s2c_b, L1_ffn_r_w1, L1_ffn_r_b1, L1_ffn_r_w2, L1_ffn_r_b2, L1_ffn_e_w1, L1_ffn_e_b1, L1_ffn_e_w2, L1_ffn_e_b2, L1_ffn_c2s_w, L1_ffn_c2s_b, L1_ffn_dec_w, L1_ffn_dec_b, L1_ffn_ln_g, L1_ffn_ln_b):
    import jax
    import jax.numpy as jnp

    def _L0_tok_ref(x, W):
        import jax, jax.numpy as jnp
        import numpy as np
        VOCAB = 50257
        D_MODEL = 256
        BATCH = 4
        SEQ = 1024
        return jnp.take(W, x, axis=0)

    def _L0_attn_ref(x, qkv_w, qkv_b, proj_w, proj_b):
        import jax, jax.numpy as jnp
        import numpy as np
        B, N, C = (2, 512, 256)
        H = 16
        D = C // H
        b, n, c = x.shape
        scale = (c // H) ** (-0.5)
        qkv = x @ qkv_w + qkv_b
        qkv = qkv.reshape(b, n, 3, H, D)
        q, k, v = jnp.moveaxis(qkv, 2, 0)
        attn = jnp.einsum('bnhd,bmhd->bhnm', q, k) * scale
        attn = jax.nn.softmax(attn, axis=-1)
        out = jnp.einsum('bhnm,bmhd->bnhd', attn, v).reshape(b, n, c)
        out = out @ proj_w + proj_b
        return out

    def _L0_ffn_ref(x, w1, b1, w2, b2):
        import jax, jax.numpy as jnp
        import numpy as np
        B, S, D = (4, 512, 256)
        N_EXPERTS, EXPERT_SIZE = (16, 64)
        WIDTH = N_EXPERTS * EXPERT_SIZE
        h = jax.nn.relu(jnp.einsum('bsd,dw->bsw', x, w1) + b1)
        return jnp.einsum('bsw,wd->bsd', h, w2) + b2

    def _L1_attn_ref(hidden_states, Wq, bq, Wv, bv, anomaly_matrix):
        import jax, jax.numpy as jnp
        import numpy as np
        HIDDEN = 256
        B, S = (8, 512)
        input_norm = jnp.linalg.norm(hidden_states, axis=-1, keepdims=True)
        scaled = hidden_states / (input_norm + 1e-09)
        q = jnp.einsum('bsh,oh->bso', scaled, Wq) + bq
        v = jnp.einsum('bsh,oh->bso', scaled, Wv) + bv
        tq = jnp.einsum('bsh,hk->bsk', q, anomaly_matrix)
        scores = jnp.einsum('bsh,bth->bst', q, tq) / jnp.sqrt(jnp.float32(HIDDEN))
        probs = jax.nn.softmax(scores, axis=-1)
        ctx = jnp.einsum('bst,bth->bsh', probs, v)
        return ctx * input_norm

    def _L1_ffn_ref(inputs_embeds, enc_w, enc_b, s2c_w, s2c_b, r_w1, r_b1, r_w2, r_b2, e_w1, e_b1, e_w2, e_b2, c2s_w, c2s_b, dec_w, dec_b, ln_g, ln_b):
        import jax, jax.numpy as jnp
        import numpy as np
        D_MODEL = 256
        HIDDEN = 512
        MOE_DIM = 64
        N_EXPERTS = 8
        TOP_K = 2
        EXP_HIDDEN = HIDDEN // 2
        B, S = (4, 512)
        b, s, _ = inputs_embeds.shape
        spikes = jax.nn.sigmoid(inputs_embeds @ enc_w + enc_b)
        cont = spikes.reshape(b * s, -1) @ s2c_w + s2c_b
        rh = jax.nn.relu(cont @ r_w1 + r_b1)
        probs = jax.nn.softmax(rh @ r_w2 + r_b2, axis=-1)
        topw, topi = jax.lax.top_k(probs, TOP_K)
        topw = topw / jnp.sum(topw, axis=-1, keepdims=True)
        comb = jnp.sum(jax.nn.one_hot(topi, N_EXPERTS, dtype=cont.dtype) * topw[..., None], axis=1)
        eh = jax.nn.relu(jnp.einsum('nd,edh->neh', cont, e_w1) + e_b1)
        eo = jnp.einsum('neh,ehd->ned', eh, e_w2) + e_b2
        moe_out = jnp.einsum('ned,ne->nd', eo, comb)
        rates = jax.nn.sigmoid(moe_out @ c2s_w + c2s_b)
        x = rates.reshape(b, s, -1)
        dec = jax.nn.sigmoid(x @ dec_w + dec_b)
        mu = jnp.mean(dec, axis=-1, keepdims=True)
        var = jnp.var(dec, axis=-1, keepdims=True)
        return (dec - mu) * jax.lax.rsqrt(var + 1e-05) * ln_g + ln_b
    h = _L0_tok_ref(x, L0_tok_W)
    h = h + _L0_attn_ref(_layernorm(h, axis=-1), L0_attn_qkv_w, L0_attn_qkv_b, L0_attn_proj_w, L0_attn_proj_b)
    h = h + _L0_ffn_ref(_layernorm(h, axis=-1), L0_ffn_w1, L0_ffn_b1, L0_ffn_w2, L0_ffn_b2)
    h = h + _L1_attn_ref(_layernorm(h, axis=-1), L1_attn_Wq, L1_attn_bq, L1_attn_Wv, L1_attn_bv, L1_attn_anomaly_matrix)
    h = h + _L1_ffn_ref(_layernorm(h, axis=-1), L1_ffn_enc_w, L1_ffn_enc_b, L1_ffn_s2c_w, L1_ffn_s2c_b, L1_ffn_r_w1, L1_ffn_r_b1, L1_ffn_r_w2, L1_ffn_r_b2, L1_ffn_e_w1, L1_ffn_e_b1, L1_ffn_e_w2, L1_ffn_e_b2, L1_ffn_c2s_w, L1_ffn_c2s_b, L1_ffn_dec_w, L1_ffn_dec_b, L1_ffn_ln_g, L1_ffn_ln_b)
    return h

_drawn_inputs = setup_inputs


def setup_inputs(seed=0):
    import zlib

    import numpy as np

    out = dict(_drawn_inputs(seed))
    spreads = {'L0_ffn_b1': (0.0, 0.298),
     'L0_ffn_b2': (0.0, 0.297),
     'L1_attn_bq': (0.0, 0.8),
     'L1_attn_bv': (0.0, 0.1),
     'L1_ffn_enc_b': (0.0, 1.587),
     'L1_ffn_s2c_b': (0.0, 0.29),
     'L1_ffn_r_b1': (0.0, 0.342),
     'L1_ffn_r_b2': (0.0, 0.273),
     'L1_ffn_e_b1': (0.0, 2.0),
     'L1_ffn_e_b2': (0.0, 0.605),
     'L1_ffn_c2s_b': (0.0, 0.372),
     'L1_ffn_dec_b': (0.0, 0.1),
     'L1_ffn_ln_g': (1.0, 0.2),
     'L1_ffn_ln_b': (0.0, 0.412)}
    factors = {'L0_attn_qkv_w': 8.0,
     'L0_attn_qkv_b': 8.0,
     'L0_attn_proj_w': 8.0,
     'L0_attn_proj_b': 4.295,
     'L1_attn_Wq': 8.0,
     'L1_attn_anomaly_matrix': 7.657,
     'L1_ffn_e_w1': 2.667}
    for name, (base, spread) in spreads.items():
        noise = np.random.default_rng([zlib.crc32(name.encode()), seed]).standard_normal(out[name].shape)
        drawn = base * np.exp(spread * noise) if base else spread * noise
        out[name] = jnp.asarray(drawn.astype(out[name].dtype))
    for name, factor in factors.items():
        out[name] = (out[name] * factor).astype(out[name].dtype)
    return out
```

```python
from contextlib import ExitStack

import concourse.bass as bass
from concourse import mybir

F32 = mybir.dt.float32
F32R = mybir.dt.float32r
I32 = mybir.dt.int32
ALU = mybir.AluOpType
ACT = mybir.ActivationFunctionType
AX = mybir.AxisListType

P = 128
BANK = 512


def first_layer(nc, x, tok_w, qkv_w, qkv_b, proj_w, proj_b, w1, b1, w2, b2, h_mid):
    B, N = x.shape
    D = tok_w.shape[1]
    KC = D // P
    TT = N // P
    TB = N // BANK
    HEADS, GH = 16, 4
    HD = D // HEADS
    G = HEADS // GH
    WIDTH = w1.shape[1]
    M1 = WIDTH // P
    SCALE = float(HD) ** -0.5
    EPS = 1e-5
    SLOTS = 10
    KR = 128
    NEG = 4 * HD
    VC = HD + 1
    STEPS = TB * TT
    UNITS = GH * TT * 2
    US = 4
    AHEAD = UNITS + 4 * US
    MAXED = (UNITS - (AHEAD - UNITS)) // US
    RING = 6
    ctx = ExitStack()
    with ctx:
        base = (nc.sbuf_base + 31) // 32 * 32
        top = [base]

        def at(name, shape, dt, offset=None):
            size = 4
            for n in shape[1:]:
                size *= n
            if offset is None:
                offset = top[0]
                top[0] += (size + 31) // 32 * 32
            return nc.alloc_sbuf_tensor_at(name, shape, dt, offset=offset)

        h = at("h", [P, TT, D], F32)
        xn_at = top[0]
        xn = at("xn", [P, TT, D], F32)
        xt_at = top[0]
        xt_hi = at("xt_hi", [P, KC, N], F32R)
        xt_lo = at("xt_lo", [P, KC, N], F32R)
        w1_raw = at("w1_raw", [P, KC, WIDTH], F32, xt_at)
        w2_raw = at("w2_raw", [P, M1, D], F32, xt_at + 4 * KC * WIDTH)
        qk_at = top[0]
        qk_hi = at("qk_hi", [P, G, N], F32R)
        qk_lo = at("qk_lo", [P, G, N], F32R)
        w1_hi = at("w1_hi", [P, KC, WIDTH], F32R, qk_at)
        w1_lo = at("w1_lo", [P, KC, WIDTH], F32R, qk_at + 4 * KC * WIDTH)
        w2_hi = at("w2_hi", [P, M1, D], F32R, qk_at + 8 * KC * WIDTH)
        w2_lo = at("w2_lo", [P, M1, D], F32R, qk_at + 8 * KC * WIDTH + 4 * M1 * D)
        v_sb = at("v_sb", [P, TT, HEADS, 2 * HD], F32)
        stack_at = top[0]
        k_stack = at("k_stack", [P, SLOTS, N], F32R)
        q_stack = at("q_stack", [P, SLOTS, N], F32R)
        hid_hi = at("hid_hi", [P, M1, N], F32R, stack_at)
        hid_lo = at("hid_lo", [P, M1, N], F32R, stack_at + 4 * M1 * N)
        p_at = top[0]
        p_sb = at("p_sb", [P, 2, GH, BANK], F32)
        qkv_raw = at("qkv_raw", [P, KC, 3 * D], F32, p_at)
        proj_raw = at("proj_raw", [P, KC, D], F32, p_at + 12 * KC * D)
        hid_f = at("hid_f", [P, 2, BANK], F32, p_at)
        ot_sb = at("ot_sb", [P, 2, BANK], F32)
        wqk_hi = at("wqk_hi", [P, KC, G, P], F32R)
        wqk_lo = at("wqk_lo", [P, KC, G, P], F32R)
        wv_hi = at("wv_hi", [P, KC, D], F32R)
        wv_lo = at("wv_lo", [P, KC, D], F32R)
        wp_hi = at("wp_hi", [P, KC, D], F32R)
        wp_lo = at("wp_lo", [P, KC, D], F32R)
        ident = at("ident", [P, P], F32)
        bv_all = at("bv_all", [P, D], F32)
        bp_all = at("bp_all", [P, D], F32)
        b2_all = at("b2_all", [P, D], F32)
        qk_b = at("qk_b", [P, G], F32)
        b1_sb = at("b1_sb", [P, M1], F32)
        idx = at("idx", [P, TT], I32)
        stats = at("stats", [P, TT, 6], F32)
        mv = at("mv", [P, TT, 2], F32)
        rstd = at("rstd", [P, TT], F32)
        std = at("std", [P, TT], F32)
        eps = at("eps", [P, 1], F32)
        mx = at("mx", [P, 2, UNITS], F32)
        mq = at("mq", [P, GH * TT], F32)
        nm_hi = at("nm_hi", [GH * TT, P], F32R)
        nm_lo = at("nm_lo", [GH * TT, P], F32R)
        rs = at("rs", [P, 4, GH], F32)
        ps = ctx.enter_context(nc.psum_tensor("ps", [P, 8, BANK], F32))

        def sem(name):
            return ctx.enter_context(nc.semaphore(name))

        w_in = sem("w_in")
        c_in = sem("c_in")
        ones_set = sem("ones_set")
        id_set = sem("id_set")
        w_split = sem("w_split")
        v_ones = sem("v_ones")
        idx_in = sem("idx_in")
        got = [sem(f"got{t}") for t in range(TT)]
        past = sem("past")
        vec = sem("vec")
        ln_var = sem("ln_var")
        ln_std = sem("ln_std")
        xn_set = sem("xn_set")
        xt_mm = sem("xt_mm")
        xt_h = sem("xt_h")
        xt_l = sem("xt_l")
        qk_mm = sem("qk_mm")
        qk_h = sem("qk_h")
        qk_l = sem("qk_l")
        v_mm = sem("v_mm")
        v_set = sem("v_set")
        rows_set = sem("rows_set")
        slot_in = [sem(f"slot_in{s}") for s in range(SLOTS)]
        w12_in = sem("w12_in")
        w12_split = sem("w12_split")
        s_mm = sem("s_mm")
        s_max = sem("s_max")
        m_set = sem("m_set")
        m_tr = sem("m_tr")
        nm_set = sem("nm_set")
        nm_in = sem("nm_in")
        st_mm = sem("st_mm")
        p_set = sem("p_set")
        pv_mm = sem("pv_mm")
        ot_set = sem("ot_set")
        ot_tr = sem("ot_tr")
        o_norm = sem("o_norm")
        hb_set = sem("hb_set")
        pr_mm = sem("pr_mm")
        h1_set = sem("h1_set")
        w1_mm = sem("w1_mm")
        hid_set = sem("hid_set")
        hid_split = sem("hid_split")
        w2_mm = sem("w2_mm")
        h2_set = sem("h2_set")
        mid_out = sem("mid_out")
        HIW = 8 * HD

        block = ctx.enter_context(nc.Block())

        def wqkv_cols(t, part):
            return t[:, :, :, part * GH * HD:(part + 1) * GH * HD]

        @block.sync
        def _(sp):
            sp.dma_start(qkv_raw[:, :, :], qkv_w.rearrange("(k p) n -> p k n", p=P)).then_inc(w_in, 16)
            sp.dma_start(proj_raw[:, :, :], proj_w.rearrange("(k p) n -> p k n", p=P)).then_inc(w_in, 16)
            with nc.allow_non_contiguous_dma("biases by partition"):
                for part in range(2):
                    sp.dma_start(qk_b[part * 64:part * 64 + 64, :],
                                 qkv_b[part * D:(part + 1) * D].rearrange("(g c) -> c g", g=G)).then_inc(c_in, 16)
                sp.dma_start(b1_sb[:, :], b1.rearrange("(m p) -> p m", p=P)).then_inc(c_in, 16)
            sp.dma_start(bv_all[:, :], qkv_b[2 * D:3 * D].partition_broadcast(P)).then_inc(c_in, 16)
            sp.dma_start(bp_all[:, :], proj_b.partition_broadcast(P)).then_inc(c_in, 16)
            sp.dma_start(b2_all[:, :], b2.partition_broadcast(P)).then_inc(c_in, 16)
            sp.sem_inc(mid_out, 16)
            with sp.Fori(0, B, 1) as b:
                sp.dma_start(idx[:, :], x[bass.ds(b, 1), :].rearrange("o (p t) -> p (o t)", p=P)).then_inc(idx_in, 16)

                def load_stacks(hd):
                    g, j, slot = hd // GH, hd % GH, hd % SLOTS
                    if hd < SLOTS:
                        sp.wait_ge(qk_l, b * G * TB + TB * (g + 1))
                    else:
                        sp.wait_ge(st_mm, b * G * 2 * STEPS + 2 * STEPS * ((hd - SLOTS) // GH + 1))
                        sp.wait_ge(pv_mm, b * G * STEPS + 1)
                    q = slice(j * HD, (j + 1) * HD)
                    k = slice(64 + j * HD, 64 + (j + 1) * HD)
                    for r, (qp, kp) in enumerate(((qk_hi, qk_hi), (qk_hi, qk_lo), (qk_lo, qk_hi), (qk_lo, qk_lo))):
                        sp.dma_start(q_stack[r * HD:(r + 1) * HD, slot, :].bitcast(F32), qp[q, g, :].bitcast(F32)).then_inc(slot_in[slot], 16)
                        sp.dma_start(k_stack[r * HD:(r + 1) * HD, slot, :].bitcast(F32), kp[k, g, :].bitcast(F32)).then_inc(slot_in[slot], 16)

                def load_neg_max(g):
                    sp.wait_ge(nm_set, b * 2 * G + 2 * g + 2)
                    s0 = g * GH % SLOTS
                    first = min(GH, SLOTS - s0)
                    for row, src in ((NEG, nm_hi), (NEG + 1, nm_lo)):
                        for lo, n, slot in ((0, first, s0), (first, GH - first, 0)):
                            if n:
                                sp.dma_start(
                                    q_stack[row:row + 1, slot:slot + n, :].bitcast(F32).rearrange("o s (t c) -> o (s t) c", c=P),
                                    src[lo * TT:(lo + n) * TT, :].bitcast(F32),
                                ).then_inc(nm_in, 16)

                for hd in range(SLOTS):
                    load_stacks(hd)
                sp.wait_ge(v_mm, b * TT + TT)
                sp.dma_start(w1_raw[:, :, :], w1.rearrange("(k p) n -> p k n", p=P)).then_inc(w12_in, 16)
                sp.dma_start(w2_raw[:, :, :], w2.rearrange("(m p) n -> p m n", p=P)).then_inc(w12_in, 16)
                load_neg_max(0)
                load_neg_max(1)
                for hd in range(SLOTS, 3 * GH + 2):
                    load_stacks(hd)
                load_neg_max(2)
                for hd in range(3 * GH + 2, HEADS):
                    load_stacks(hd)
                load_neg_max(3)
                sp.wait_ge(h2_set, b * TT + TT)
                sp.dma_start(h_mid[bass.ds(b, 1)].rearrange("o (p t) d -> p (o t) d", p=P), h[:, :, :]).then_inc(mid_out, 16)
            sp.wait_ge(mid_out, 16 * B + 16)

        NMD = [2 * 16 * (2 if (g * GH % SLOTS) + GH > SLOTS else 1) for g in range(G)]
        NMC = [sum(NMD[:g + 1]) for g in range(G)]

        @block.gpsimd
        def _(pool):
            pool.memset(ident[:, :], 0.0).then_inc(ones_set, 1)
            pool.wait_ge(ones_set, 1)
            pool.affine_select(out=ident[:, :], in_=ident[:, :], compare_op=ALU.not_equal, fill=1.0, base=0,
                               pattern=[[-1, P]], channel_multiplier=1).then_inc(id_set, 1)
            pool.memset(v_sb[:, :, :, HD:2 * HD], 0.0).then_inc(v_ones, 1)
            pool.wait_ge(v_ones, 1)
            pool.memset(v_sb[:, :, :, HD:HD + 1], 1.0).then_inc(v_ones, 1)
            with pool.Fori(0, B, 1) as b:
                pool.wait_ge(idx_in, b * 16 + 16)
                pool.wait_ge(mid_out, b * 16 + 16)
                pool.sem_inc(past, 1)
                for t in range(TT):
                    pool.indirect_dma_start(out=h[:, t, :], out_offset=None, in_=tok_w,
                                            in_offset=bass.IndirectOffsetOnAxis(ap=idx[:, t:t + 1], axis=0)
                                            ).then_inc(got[t], 16)
                pool.wait_ge(v_ones, 2)
                for n, (s0, s1) in enumerate(((0, GH), (GH, SLOTS))):
                    pool.sem_inc(past, 1)
                    pool.memset(q_stack[NEG:KR, s0:s1, :].bitcast(I32), 0).then_inc(rows_set, 1)
                    pool.wait_ge(rows_set, b * 6 + 2 * n + 1)
                    pool.sem_inc(past, 1)
                    pool.memset(k_stack[NEG:KR, s0:s1, :].bitcast(F32), 1.0).then_inc(rows_set, 1)
                    pool.wait_ge(rows_set, b * 6 + 2 * n + 2)
                pool.wait_ge(xn_set, b * 2 * TT + TT)
                pool.wait_ge(c_in, 16 * 6)
                pool.tensor_tensor(h[:, :, :], h[:, :, :], bp_all[:, :].unsqueeze(1).broadcast_to([P, TT, D]),
                                   ALU.add).then_inc(hb_set, 1)
                pool.wait_ge(st_mm, b * G * 2 * STEPS + 2 * STEPS)
                pool.wait_ge(hb_set, b * 2 + 1)
                pool.sem_inc(past, 1)
                pool.memset(q_stack[NEG:NEG + 2, 0:GH, :].bitcast(F32), 0.0).then_inc(rows_set, 1)
                pool.wait_ge(rows_set, b * 6 + 5)
                pool.wait_ge(st_mm, b * G * 2 * STEPS + 4 * STEPS)
                pool.sem_inc(past, 1)
                pool.memset(q_stack[NEG:NEG + 2, GH:HEADS - SLOTS, :].bitcast(F32), 0.0).then_inc(rows_set, 1)
                pool.wait_ge(w12_in, b * 32 + 32)
                for s in range(SLOTS):
                    uses = 2 if s < HEADS - SLOTS else 1
                    pool.wait_ge(slot_in[s], b * uses * HIW + uses * HIW)
                pool.wait_ge(rows_set, b * 6 + 6)
                pool.sem_inc(past, 1)
                pool.tensor_copy(w1_hi[:, :, :], w1_raw[:, :, :]).then_inc(w12_split, 1)
                pool.tensor_copy(w2_hi[:, :, :], w2_raw[:, :, :]).then_inc(w12_split, 1)
                pool.wait_ge(w12_split, b * 4 + 2)
                pool.tensor_tensor(w1_lo[:, :, :], w1_raw[:, :, :], w1_hi[:, :, :].bitcast(F32), ALU.subtract).then_inc(w12_split, 1)
                pool.tensor_tensor(w2_lo[:, :, :], w2_raw[:, :, :], w2_hi[:, :, :].bitcast(F32), ALU.subtract).then_inc(w12_split, 1)
                pool.wait_ge(xn_set, b * 2 * TT + 2 * TT)
                pool.tensor_tensor(h[:, :, :], h[:, :, :], b2_all[:, :].unsqueeze(1).broadcast_to([P, TT, D]),
                                   ALU.add).then_inc(hb_set, 1)

        PB = (0, 1, 6, 7)
        XT_N = 3 * 2 * TB

        @block.scalar
        def _(act):
            act.wait_ge(c_in, 16 * 6)
            with act.Fori(0, B, 1) as b:
                def std_of(n):
                    act.wait_ge(ln_var, b * 2 + n)
                    act.activation(std[:, :], mv[:, :, 1], ACT.Sqrt, bias=eps[:, 0:1]).then_inc(ln_std, 1)

                def xt_parts(n):
                    for u in range(KC * TB):
                        tb, kc = u // KC, u % KC
                        act.wait_ge(xt_mm, b * XT_N + n * KC * TB + u + 1)
                        act.activation(xt_hi[:, kc, tb * BANK:(tb + 1) * BANK], ps[:, 2 + u, :], ACT.Copy).then_inc(xt_h, 1)

                std_of(1)
                xt_parts(0)
                for u in range(G * TB):
                    g, tb = u // TB, u % TB
                    act.wait_ge(qk_mm, b * G * TB + u + 1)
                    act.activation(qk_hi[:, g, tb * BANK:(tb + 1) * BANK], ps[:, PB[u % 4], :], ACT.Identity,
                                   bias=qk_b[:, g:g + 1]).then_inc(qk_h, 1)

                def copy_out(o):
                    act.wait_ge(pv_mm, b * G * STEPS + (o + 1) * TT)
                    if o >= 2:
                        act.wait_ge(ot_tr, b * G * TB + o - 1)
                    act.activation(ot_sb[:, o % 2, :], ps[:, 6 + o % 2, :], ACT.Copy).then_inc(ot_set, 1)

                for g in range(G):
                    for i in range(STEPS):
                        n = g * STEPS + i
                        for jp in range(2):
                            act.wait_ge(st_mm, b * G * 2 * STEPS + 2 * n + jp + 1)
                            if n >= 2:
                                act.wait_ge(pv_mm, b * G * STEPS + n - 1)
                            act.activation(p_sb[:, n % 2, 2 * jp:2 * jp + 2, :], ps[:, 2 + 2 * jp:4 + 2 * jp, :],
                                           ACT.Exp, scale=SCALE).then_inc(p_set, 1)
                        if n >= TT and n % TT == 1:
                            copy_out(n // TT - 1)
                copy_out(G * TB - 1)
                act.wait_ge(w12_split, b * 4 + 4)
                xt_parts(1)
                std_of(2)
                xt_parts(2)
                for u in range(M1 * TB):
                    m, tb = u % M1, u // M1
                    act.wait_ge(w1_mm, b * M1 * TB + u + 1)
                    if u >= 2:
                        act.wait_ge(hid_split, b * 2 * M1 * TB + 2 * (u - 1))
                    act.activation(hid_f[:, u % 2, :], ps[:, PB[u % 4], :], ACT.Relu, bias=b1_sb[:, m:m + 1]).then_inc(hid_set, 1)

        @block.vector
        def _(dve):
            dve.memset(eps[:, :], EPS)
            dve.wait_ge(w_in, 32)
            whole = []
            for kc in range(KC):
                for part in range(2):
                    whole.append((wqk_hi[:, kc, :, part * 64:(part + 1) * 64], wqk_lo[:, kc, :, part * 64:(part + 1) * 64],
                                  qkv_raw[:, kc, part * D:(part + 1) * D].rearrange("p (g c) -> p g c", g=G)))
            whole.append((wv_hi[:, :, :], wv_lo[:, :, :], qkv_raw[:, :, 2 * D:3 * D]))
            whole.append((wp_hi[:, :, :], wp_lo[:, :, :], proj_raw[:, :, :]))
            for hi, _lo, raw in whole:
                dve.tensor_copy(hi, raw).then_inc(w_split, 1)
            dve.wait_ge(w_split, len(whole))
            for hi, lo, raw in whole:
                dve.tensor_tensor(lo, raw, hi.bitcast(F32), ALU.subtract).then_inc(w_split, 1)
            dve.wait_ge(c_in, 16 * 6)
            with dve.Fori(0, B, 1) as b:
                chain = [0]
                CHAIN = 2 * (2 * TT - 1 + 1) + G * TB

                def then(ins):
                    chain[0] += 1
                    ins.then_inc(vec, 1)

                def settle():
                    dve.wait_ge(vec, b * CHAIN + chain[0])

                def normalise(n):
                    for t in range(TT):
                        if n == 1:
                            dve.wait_ge(got[t], b * 16 + 16)
                        then(dve.bn_stats(stats[:, t, :], h[:, t, :]))
                    settle()
                    dve.sem_inc(past, 1)
                    for t in range(TT):
                        ins = dve.bn_aggr(mv[:, t, :], stats[:, t, :])
                        if t == TT - 1:
                            ins.then_inc(ln_var, 1)
                        else:
                            then(ins)
                    settle()
                    dve.wait_ge(ln_std, b * 2 + n)
                    then(dve.reciprocal(rstd[:, :], std[:, :]))
                    settle()
                    for t in range(TT):
                        dve.tensor_scalar(xn[:, t, :], h[:, t, :], mv[:, t, 0:1], rstd[:, t:t + 1],
                                          ALU.subtract, ALU.mult).then_inc(xn_set, 1)

                def xt_rest(n):
                    for u in range(KC * TB):
                        tb, kc = u // KC, u % KC
                        cols = slice(tb * BANK, (tb + 1) * BANK)
                        dve.wait_ge(xt_h, b * XT_N + n * KC * TB + u + 1)
                        dve.tensor_tensor(xt_lo[:, kc, cols], ps[:, 2 + u, :], xt_hi[:, kc, cols].bitcast(F32),
                                          ALU.subtract).then_inc(xt_l, 1)

                normalise(1)
                xt_rest(0)
                for u in range(G * TB):
                    g, tb = u // TB, u % TB
                    cols = slice(tb * BANK, (tb + 1) * BANK)
                    dve.wait_ge(qk_h, b * G * TB + u + 1)
                    dve.scalar_tensor_tensor(out=qk_lo[:, g, cols], in0=ps[:, PB[u % 4], :], scalar=qk_b[:, g:g + 1],
                                             in1=qk_hi[:, g, cols].bitcast(F32), op0=ALU.add, op1=ALU.subtract).then_inc(qk_l, 1)
                dve.wait_ge(v_ones, 2)
                for t in range(TT):
                    dve.wait_ge(v_mm, b * TT + t + 1)
                    dve.tensor_tensor(v_sb[:, t, :, 0:HD], ps[:, 2 + t % 4, 0:D].rearrange("p (a c) -> p a c", c=HD),
                                      bv_all[:, :].rearrange("p (a c) -> p a c", c=HD), ALU.add).then_inc(v_set, 1)

                def max_unit(u):
                    g, n = u // UNITS, u % UNITS
                    dve.wait_ge(s_mm, b * G * UNITS + u + 1)
                    dve.tensor_reduce(mx[:, g % 2, n:n + 1], ps[:, u % (RING if u < AHEAD else 2), :], AX.X,
                                      ALU.max).then_inc(s_max, 1)

                def group_max(g):
                    dve.wait_ge(s_max, b * G * UNITS + (g + 1) * UNITS)
                    pair = mx[:, g % 2, :].rearrange("p (n two) -> p n two", two=2)
                    dve.tensor_tensor(mq[:, :], pair[:, :, 0], pair[:, :, 1], ALU.max).then_inc(m_set, 1)

                def neg_max(g):
                    if g:
                        dve.wait_ge(nm_in, b * NMC[-1] + NMC[g - 1])
                    dve.wait_ge(m_tr, b * G + g + 1)
                    dve.tensor_scalar(nm_hi[:, :], ps[0:GH * TT, 0 if g else 7, 0:P], -1.0, None, ALU.mult).then_inc(nm_set, 1)
                    dve.wait_ge(nm_set, b * 2 * G + 2 * g + 1)
                    dve.scalar_tensor_tensor(out=nm_lo[:, :], in0=ps[0:GH * TT, 0 if g else 7, 0:P], scalar=-1.0,
                                             in1=nm_hi[:, :].bitcast(F32), op0=ALU.mult, op1=ALU.subtract).then_inc(nm_set, 1)

                def norm_out(o):
                    g, qb = o // TB, o % TB
                    dve.wait_ge(ot_tr, b * G * TB + o + 1)
                    if o:
                        dve.wait_ge(o_norm, b * G * TB + o)
                    view = ps[:, 6 + o % 2, :].rearrange("p (t j c) -> p t j c", t=4, j=GH)
                    then(dve.reciprocal(rs[:, :, :], view[:, :, :, HD]))
                    settle()
                    dve.tensor_tensor(xn[:, 4 * qb:4 * qb + 4, g * GH * HD:(g + 1) * GH * HD].rearrange(
                                          "p t (j c) -> p t j c", j=GH),
                                      view[:, :, :, 0:HD], rs[:, :, :].unsqueeze(3).broadcast_to([P, 4, GH, HD]),
                                      ALU.mult).then_inc(o_norm, 1)

                for u in range(AHEAD):
                    max_unit(u)
                    if u == UNITS - 1:
                        group_max(0)
                    if u == UNITS + 3:
                        neg_max(0)
                for g in range(G):
                    for i in range(STEPS):
                        n = g * STEPS + i
                        for u in range(AHEAD + US * n, min(AHEAD + US * (n + 1), G * UNITS)):
                            max_unit(u)
                        if g + 1 < G and i == MAXED - 1:
                            group_max(g + 1)
                        if g + 1 < G and i == MAXED:
                            neg_max(g + 1)
                        if n >= TT and n % TT == 3:
                            norm_out(n // TT - 1)
                norm_out(G * TB - 1)
                xt_rest(1)
                dve.wait_ge(hb_set, b * 2 + 1)
                for t in range(TT):
                    dve.wait_ge(pr_mm, b * TT + t + 1)
                    dve.tensor_tensor(h[:, t, :], ps[:, PB[t % 4], 0:D], h[:, t, :], ALU.add).then_inc(h1_set, 1)
                dve.wait_ge(h1_set, b * TT + TT)
                normalise(2)
                xt_rest(2)
                for u in range(M1 * TB):
                    m, tb = u % M1, u // M1
                    cols = slice(tb * BANK, (tb + 1) * BANK)
                    dve.wait_ge(hid_set, b * M1 * TB + u + 1)
                    dve.tensor_copy(hid_hi[:, m, cols], hid_f[:, u % 2, :]).then_inc(hid_split, 1)
                    dve.wait_ge(hid_split, b * 2 * M1 * TB + 2 * u + 1)
                    dve.tensor_tensor(hid_lo[:, m, cols], hid_f[:, u % 2, :], hid_hi[:, m, cols].bitcast(F32),
                                      ALU.subtract).then_inc(hid_split, 1)
                dve.wait_ge(hb_set, b * 2 + 2)
                for t in range(TT):
                    dve.wait_ge(w2_mm, b * TT + t + 1)
                    dve.tensor_tensor(h[:, t, :], ps[:, 2 + t % 4, 0:D], h[:, t, :], ALU.add).then_inc(h2_set, 1)
                assert chain[0] == CHAIN, chain

        @block.tensor
        def _(pe):
            pe.wait_ge(id_set, 1)
            pe.wait_ge(w_split, 2 * 6)
            with pe.Fori(0, B, 1) as b:
                def transposes(n, ready):
                    for tb in range(TB):
                        for kc in range(KC):
                            for i in range(4):
                                t = 4 * tb + i
                                if kc == 0 or n == 1:
                                    ready(t)
                                ins = pe.transpose(ps[:, 2 + KC * tb + kc, i * P:(i + 1) * P], xn[:, t, kc * P:(kc + 1) * P],
                                                   ident[:, :])
                            ins.then_inc(xt_mm, 1)

                def product(out, pairs):
                    for i, (w, a) in enumerate(pairs):
                        ins = pe.matmul(out, w, a, start=(i == 0), stop=(i == len(pairs) - 1))
                    return ins

                def three(hi_a, lo_a, hi_b, lo_b):
                    return [(hi_a, hi_b), (hi_a, lo_b), (lo_a, hi_b)]

                transposes(0, lambda t: pe.wait_ge(xn_set, b * 2 * TT + t + 1))
                for u in range(G * TB):
                    g, tb = u // TB, u % TB
                    cols = slice(tb * BANK, (tb + 1) * BANK)
                    if u < TB:
                        pe.wait_ge(xt_h, b * XT_N + KC * (tb + 1))
                        pe.wait_ge(xt_l, b * XT_N + KC * (tb + 1))
                    if u >= 4:
                        pe.wait_ge(qk_l, b * G * TB + u - 3)
                    product(ps[:, PB[u % 4], :],
                            [x_ for kc in range(KC) for x_ in three(wqk_hi[:, kc, g, :], wqk_lo[:, kc, g, :],
                                                                    xt_hi[:, kc, cols], xt_lo[:, kc, cols])]).then_inc(qk_mm, 1)
                for t in range(TT):
                    rows = slice(t * P, (t + 1) * P)
                    if t >= 4:
                        pe.wait_ge(v_set, b * TT + t - 3)
                    product(ps[:, 2 + t % 4, 0:D],
                            [x_ for kc in range(KC) for x_ in three(xt_hi[:, kc, rows], xt_lo[:, kc, rows],
                                                                    wv_hi[:, kc, :], wv_lo[:, kc, :])]).then_inc(v_mm, 1)

                def score_unit(u):
                    hd, t, kh = u // (2 * TT), u // 2 % TT, u % 2
                    slot = hd % SLOTS
                    if u % (2 * TT) == 0:
                        uses = 2 if slot < HEADS - SLOTS else 1
                        pe.wait_ge(slot_in[slot], b * uses * HIW + (hd // SLOTS + 1) * HIW)
                        pe.wait_ge(rows_set, b * 6 + (2 if hd < GH else 4 if hd < SLOTS else 5 if hd < SLOTS + GH else 6))
                    if u == 0:
                        pe.wait_ge(qk_l, b * G * TB + G * TB)
                        pe.wait_ge(v_set, b * TT + TT)
                    ring = RING if u < AHEAD else 2
                    if u >= ring:
                        pe.wait_ge(s_max, b * G * UNITS + u - ring + 1)
                    pe.matmul(ps[:, u % ring, :], q_stack[0:KR, slot, t * P:(t + 1) * P],
                              k_stack[0:KR, slot, kh * BANK:(kh + 1) * BANK], start=True, stop=True).then_inc(s_mm, 1)

                def turn_max(g):
                    pe.wait_ge(m_set, b * G + g + 1)
                    if g:
                        last = AHEAD + US * ((g - 1) * STEPS + MAXED + 1) - 2
                        pe.wait_ge(s_max, b * G * UNITS + min(last + 1, G * UNITS - 1))
                    pe.transpose(ps[0:GH * TT, 0 if g else 7, 0:P], mq[:, :], ident[:, :]).then_inc(m_tr, 1)

                def scores_t(g, i, jp):
                    qb, kt = i // TT, i % TT
                    n = g * STEPS + i
                    if i == 0 and jp == 0:
                        pe.wait_ge(nm_in, b * NMC[-1] + NMC[g])
                    if n == 0 and jp == 0:
                        pe.wait_ge(s_max, b * G * UNITS + AHEAD)
                    if n >= 1:
                        pe.wait_ge(p_set, b * G * 2 * STEPS + 2 * n + jp - 1)
                    for j in (2 * jp, 2 * jp + 1):
                        slot = (g * GH + j) % SLOTS
                        ins = pe.matmul(ps[:, 2 + j, :], k_stack[0:KR, slot, kt * P:(kt + 1) * P],
                                        q_stack[0:KR, slot, qb * BANK:(qb + 1) * BANK], start=True, stop=True)
                    ins.then_inc(st_mm, 1)

                def values(g, i):
                    qb, kt = i // TT, i % TT
                    n, o = g * STEPS + i, g * TB + qb
                    if kt == 0 and o >= 2:
                        pe.wait_ge(o_norm, b * G * TB + o - 1)
                    pe.wait_ge(p_set, b * G * 2 * STEPS + 2 * n + 2)
                    for j in range(GH):
                        ins = pe.matmul(ps[32 * j:32 * j + 2 * HD, 6 + o % 2, :], v_sb[:, kt, g * GH + j, :],
                                        p_sb[:, n % 2, j, :], start=(kt == 0), stop=(kt == TT - 1))
                    ins.then_inc(pv_mm, 1)

                def turn_out(o):
                    pe.wait_ge(ot_set, b * G * TB + o + 1)
                    for t in range(4):
                        ins = pe.transpose(ps[:, 6 + o % 2, t * P:(t + 1) * P], ot_sb[:, o % 2, t * P:(t + 1) * P], ident[:, :])
                    ins.then_inc(ot_tr, 1)

                for u in range(AHEAD):
                    score_unit(u)
                    if u == UNITS + 3:
                        turn_max(0)
                for g in range(G):
                    for i in range(STEPS):
                        n = g * STEPS + i
                        units = list(range(AHEAD + US * n, min(AHEAD + US * (n + 1), G * UNITS)))
                        for jp in range(2):
                            if units:
                                if g + 1 < G and i == MAXED + 1 and jp == 0:
                                    pe.wait_ge(nm_set, b * 2 * G + 2 * g + 4)
                                score_unit(units[jp])
                            scores_t(g, i, jp)
                        for u in units[2:]:
                            score_unit(u)
                        if g + 1 < G and i == MAXED:
                            turn_max(g + 1)
                        if n:
                            values((n - 1) // STEPS, (n - 1) % STEPS)
                        if n >= TT and n % TT == 3:
                            turn_out(n // TT - 1)
                values(G - 1, STEPS - 1)
                turn_out(G * TB - 1)

                transposes(1, lambda t: pe.wait_ge(o_norm, b * G * TB + (G - 1) * TB + t // 4 + 1))
                pe.wait_ge(xt_h, b * XT_N + 2 * KC * TB)
                pe.wait_ge(xt_l, b * XT_N + 2 * KC * TB)
                for t in range(TT):
                    rows = slice(t * P, (t + 1) * P)
                    if t >= 4:
                        pe.wait_ge(h1_set, b * TT + t - 3)
                    product(ps[:, PB[t % 4], 0:D],
                            [x_ for kc in range(KC) for x_ in three(xt_hi[:, kc, rows], xt_lo[:, kc, rows],
                                                                    wp_hi[:, kc, :], wp_lo[:, kc, :])]).then_inc(pr_mm, 1)
                transposes(2, lambda t: pe.wait_ge(xn_set, b * 2 * TT + TT + t + 1))
                pe.wait_ge(w12_split, b * 4 + 4)
                for u in range(M1 * TB):
                    m, tb = u % M1, u // M1
                    cols = slice(tb * BANK, (tb + 1) * BANK)
                    if m == 0:
                        pe.wait_ge(xt_h, b * XT_N + 2 * KC * TB + KC * (tb + 1))
                        pe.wait_ge(xt_l, b * XT_N + 2 * KC * TB + KC * (tb + 1))
                    if u >= 4:
                        pe.wait_ge(hid_set, b * M1 * TB + u - 3)
                    mc = slice(m * P, (m + 1) * P)
                    product(ps[:, PB[u % 4], :],
                            [x_ for kc in range(KC) for x_ in three(w1_hi[:, kc, mc], w1_lo[:, kc, mc],
                                                                    xt_hi[:, kc, cols], xt_lo[:, kc, cols])]).then_inc(w1_mm, 1)
                for t in range(TT):
                    rows = slice(t * P, (t + 1) * P)
                    if t % 4 == 0:
                        pe.wait_ge(hid_split, b * 2 * M1 * TB + 2 * M1 * (t // 4 + 1))
                    if t >= 4:
                        pe.wait_ge(h2_set, b * TT + t - 3)
                    product(ps[:, 2 + t % 4, 0:D],
                            [x_ for m in range(M1) for x_ in three(hid_hi[:, m, rows], hid_lo[:, m, rows],
                                                                   w2_hi[:, m, :], w2_lo[:, m, :])]).then_inc(w2_mm, 1)


def second_layer(nc, h_mid, wq, bq, wv, bv, anomaly, enc_w, enc_b, s2c_w, s2c_b, r_w1, r_b1, r_w2, r_b2, e_w1, e_b1, e_w2,
          e_b2, c2s_w, c2s_b, dec_w, dec_b, ln_g, ln_b, out):
    B, N, D = h_mid.shape
    KC = D // P
    TT = N // P
    TB = N // BANK
    HID = enc_w.shape[1]
    MH = HID // P
    C = s2c_w.shape[1]
    E = r_w2.shape[1]
    EH = e_w1.shape[2] // P
    PAIRS = E // 2
    SCALE = float(D) ** -0.5
    EPS = 1e-5
    ctx = ExitStack()
    with ctx:
        base = (nc.sbuf_base + 31) // 32 * 32
        top = [base]

        def at(name, shape, dt, offset=None):
            size = 4
            for n in shape[1:]:
                size *= n
            if offset is None:
                offset = top[0]
                top[0] += (size + 31) // 32 * 32
            return nc.alloc_sbuf_tensor_at(name, shape, dt, offset=offset)

        h = at("u_h", [P, TT, D], F32)
        xn = at("u_xn", [P, TT, D], F32)
        xt_hi = at("u_xt_hi", [P, KC, N], F32R)
        xt_lo = at("u_xt_lo", [P, KC, N], F32R)
        raw_at = top[0]
        qt_hi = at("qt_hi", [P, KC, N], F32R)
        qt_lo = at("qt_lo", [P, KC, N], F32R)
        tq_hi = at("tq_hi", [P, KC, N], F32R)
        tq_lo = at("tq_lo", [P, KC, N], F32R)
        v_f = at("v_f", [P, TT, D], F32)
        v_hi = at("v_hi", [P, TT, D], F32R)
        v_lo = at("v_lo", [P, TT, D], F32R)
        pr = at("pr", [P, 2, N], F32)
        pt_hi = at("pt_hi", [P, 2, TT, P], F32R)
        pt_lo = at("pt_lo", [P, 2, TT, P], F32R)
        end = top[0]
        top[0] = raw_at
        sp_hi = at("sp_hi", [P, MH, N], F32R)
        sp_lo = at("sp_lo", [P, MH, N], F32R)
        rt_hi, rt_lo = (nc.alloc_sbuf_tensor_at(n, [P, MH, N], F32R, offset=raw_at + i * 4 * MH * N)
                        for i, n in enumerate(("rt_hi", "rt_lo")))
        cs = at("cs", [P, N], F32R)
        rs = at("u_rs", [P, N], F32R)
        eh = at("eh", [P, 8, BANK], F32)
        cb = at("cb", [P, 2, BANK], F32)
        y = at("y", [P, BANK], F32)
        ysum = at("ysum", [P, TB, BANK], F32)
        ys_hi = at("ys_hi", [P, N], F32R)
        ys_lo = at("ys_lo", [P, N], F32R)
        dd = xn
        assert top[0] <= end, (top[0], end)
        top[0] = raw_at
        wq_raw = at("wq_raw", [P, KC, D], F32)
        wv_raw = at("wv_raw", [P, KC, D], F32)
        an_raw = at("an_raw", [P, KC, D], F32)
        top[0] = end
        f_sb = at("f_sb", [P, 2, BANK], F32)
        ch = at("ch", [P, BANK], F32R)
        wqt_hi = at("wqt_hi", [P, KC, D], F32R)
        wqt_lo = at("wqt_lo", [P, KC, D], F32R)
        wvt_hi = at("wvt_hi", [P, KC, D], F32R)
        wvt_lo = at("wvt_lo", [P, KC, D], F32R)
        an_hi = at("an_hi", [P, KC, D], F32R)
        an_lo = at("an_lo", [P, KC, D], F32R)
        enc_hi = at("enc_hi", [P, KC, HID], F32R)
        enc_lo = at("enc_lo", [P, KC, HID], F32R)
        s2c_hi = at("s2c_hi", [P, MH, 2, C], F32R)
        s2c_lo = at("s2c_lo", [P, MH, 2, C], F32R)
        rw1_hi = at("rw1_hi", [P, 2, C], F32R)
        rw1_lo = at("rw1_lo", [P, 2, C], F32R)
        rw2_hi = at("rw2_hi", [P, E], F32R)
        rw2_lo = at("rw2_lo", [P, E], F32R)
        ew1_hi = at("ew1_hi", [P, E, EH * P], F32R)
        ew1_lo = at("ew1_lo", [P, E, EH * P], F32R)
        ew2_sb = at("ew2_sb", [P, E, EH, C], F32)
        c2s_hi = at("c2s_hi", [P, HID], F32R)
        c2s_lo = at("c2s_lo", [P, HID], F32R)
        dec_hi = at("dec_hi", [P, MH, D], F32R)
        dec_lo = at("dec_lo", [P, MH, D], F32R)
        ident = at("u_ident", [P, P], F32)
        bv_all = at("u_bv", [P, D], F32)
        decb_all = at("decb_all", [P, D], F32)
        g_all = at("g_all", [P, D], F32)
        lnb_all = at("lnb_all", [P, D], F32)
        rb2_all = at("rb2_all", [P, E], F32)
        bq_sb = at("bq_sb", [P, KC], F32)
        encb = at("encb", [P, MH], F32)
        s2cb = at("s2cb", [P, 1], F32)
        rb1 = at("rb1", [P, 1], F32)
        eb1 = at("eb1", [P, E, EH], F32)
        eb2 = at("eb2", [P, PAIRS], F32)
        c2sb = at("c2sb", [P, MH], F32)
        desc = at("desc", [P, E], F32)
        stats = at("u_stats", [P, TT, 6], F32)
        mv = at("u_mv", [P, TT, 2], F32)
        rstd = at("u_rstd", [P, TT], F32)
        std = at("u_std", [P, TT], F32)
        eps = at("u_eps", [P, 1], F32)
        nrc = at("nrc", [P, TT], F32)
        nrm = at("nrm", [P, TT], F32)
        nrd = at("nrd", [P, TT], F32)
        rn = at("rn", [P, TT], F32)
        smax = at("smax", [P, TT], F32)
        nb = at("nb", [P, TT], F32)
        sums = at("sums", [P, TT], F32)
        rsum = at("rsum", [P, TT], F32)
        cf = at("cf", [P, TT], F32)
        small = [at(f"small{i}", [P, TT, E], F32) for i in range(6)]
        gate_at = top[0]
        gate_w = at("gate_w", [P, TT, E, C], F32)
        gate_end = top[0]
        top[0] = gate_at
        enc_raw = at("enc_raw", [P, KC, HID], F32)
        ew1_raw = at("ew1_raw", [P, E, EH * P], F32)
        dec_raw = at("dec_raw", [P, MH, D], F32)
        assert top[0] <= gate_end
        top[0] = gate_end
        s2c_raw = at("s2c_raw", [P, MH, C], F32)
        rw1_raw = at("rw1_raw", [P, C], F32)
        rw2_raw = at("rw2_raw", [P, E], F32)
        c2s_raw = at("c2s_raw", [P, HID], F32)
        tiny = [at(f"tiny{i}", [P, TT], F32) for i in range(5)]
        ps = ctx.enter_context(nc.psum_tensor("u_ps", [P, 8, BANK], F32))

        def sem(name):
            return ctx.enter_context(nc.semaphore("u_" + name))

        raw_in = sem("raw_in")
        raw2_in = sem("raw2_in")
        bq_in = sem("bq_in")
        bv_in = sem("bv_in")
        f_hi = sem("f_hi")
        f_lo = sem("f_lo")
        c_in = sem("c_in")
        id0 = sem("id0")
        id_set = sem("id_set")
        wt_mm = sem("wt_mm")
        w_hi = sem("w_hi")
        w_set = sem("w_set")
        h_in = sem("h_in")
        past = sem("past")
        vec = sem("vec")
        ln_var = sem("ln_var")
        ln_std = sem("ln_std")
        n_set = sem("n_set")
        xn_set = sem("xn_set")
        xt_mm = sem("xt_mm")
        xt_h = sem("xt_h")
        xt_l = sem("xt_l")
        q_mm = sem("q_mm")
        q_h = sem("q_h")
        q_l = sem("q_l")
        v_mm = sem("v_mm")
        v_set = sem("v_set")
        v_parts = sem("v_parts")
        s_mm = sem("s_mm")
        nb_set = sem("nb_set")
        p_set = sem("p_set")
        pt_mm = sem("pt_mm")
        pt_h = sem("pt_h")
        pt_l = sem("pt_l")
        pv_mm = sem("pv_mm")
        h_set = sem("h_set")
        f_mm = sem("f_mm")
        f_set = sem("f_set")
        f_split = sem("f_split")
        lg_mm = sem("lg_mm")
        lg_set = sem("lg_set")
        eg_set = sem("eg_set")
        comb_set = sem("comb_set")
        gate_set = sem("gate_set")
        cb_mm = sem("cb_mm")
        cb_set = sem("cb_set")
        e1_mm = sem("e1_mm")
        eh_set = sem("eh_set")
        e2_mm = sem("e2_mm")
        y_set = sem("y_set")
        ys_set = sem("ys_set")
        de_mm = sem("de_mm")
        de_set = sem("de_set")
        dd_set = sem("dd_set")
        hb_set = sem("hb_set")
        out_set = sem("out_set")
        stored = sem("stored")
        RAWS = 3
        RAWS2 = 11
        CONSTS = 14
        FU = 2 * TB * MH + 2 * TB
        PB = (0, 1, 6, 7)

        def split_list():
            jobs = [(enc_hi[:, :, :], enc_lo[:, :, :], enc_raw[:, :, :])]
            for i in range(2):
                jobs.append((s2c_hi[:, :, i, :], s2c_lo[:, :, i, :], s2c_raw[:, :, :]))
                jobs.append((rw1_hi[:, i, :], rw1_lo[:, i, :], rw1_raw[:, :]))
            jobs.append((rw2_hi[:, :], rw2_lo[:, :], rw2_raw[:, :]))
            jobs.append((ew1_hi[:, :, :], ew1_lo[:, :, :], ew1_raw[:, :, :]))
            jobs.append((c2s_hi[:, :], c2s_lo[:, :], c2s_raw[:, :]))
            jobs.append((dec_hi[:, :, :], dec_lo[:, :, :], dec_raw[:, :, :]))
            return jobs

        SPLITS = 3
        SPLITS2 = len(split_list())

        block = ctx.enter_context(nc.Block())

        @block.sync
        def _(sp):
            def load(dst, src, s=raw_in):
                sp.dma_start(dst, src).then_inc(s, 16)

            load(wq_raw[:, :, :], wq.rearrange("(k p) n -> p k n", p=P))
            load(wv_raw[:, :, :], wv.rearrange("(k p) n -> p k n", p=P))
            load(an_raw[:, :, :], anomaly.rearrange("(k p) n -> p k n", p=P))
            load(bv_all[:, :], bv.partition_broadcast(P), bv_in)
            sp.sem_inc(stored, 16)
            with sp.Fori(0, B, 1) as b:
                sp.wait_ge(stored, b * 16 + 16)
                sp.dma_start(h[:, :, :], h_mid[bass.ds(b, 1)].rearrange("o (p t) d -> p (o t) d", p=P)).then_inc(h_in, 16)
                sp.wait_ge(out_set, b * TT + TT)
                sp.dma_start(out[bass.ds(b, 1)].rearrange("o (p t) d -> p (o t) d", p=P), h[:, :, :]).then_inc(stored, 16)
            sp.wait_ge(stored, 16 * B + 16)

        @block.gpsimd
        def _(pool):
            pool.memset(ident[:, :], 0.0).then_inc(id0, 1)
            pool.wait_ge(id0, 1)
            pool.affine_select(out=ident[:, :], in_=ident[:, :], compare_op=ALU.not_equal, fill=1.0, base=0,
                               pattern=[[-1, P]], channel_multiplier=1).then_inc(id_set, 1)
            pool.iota(desc[:, :], pattern=[[-1, E]], base=E, channel_multiplier=0,
                      allow_small_or_imprecise_dtypes=True).then_inc(id_set, 1)
            pool.wait_ge(raw2_in, 16 * RAWS2)
            for hi, _lo, raw in split_list():
                pool.tensor_copy(hi, raw).then_inc(f_hi, 1)
            pool.wait_ge(f_hi, SPLITS2)
            for hi, lo, raw in split_list():
                pool.tensor_tensor(lo, raw, hi.bitcast(F32), ALU.subtract).then_inc(f_lo, 1)
            pool.wait_ge(f_lo, SPLITS2)
            pool.wait_ge(c_in, 16 * CONSTS)
            with pool.Fori(0, B, 1) as b:
                pool.wait_ge(comb_set, b + 1)
                pool.sem_inc(past, 1)
                for tb in range(TB):
                    tiles = slice(4 * tb, 4 * tb + 4)
                    pool.tensor_copy(gate_w[:, tiles, :, :], small[5][:, tiles, :].unsqueeze(3).broadcast_to(
                        [P, 4, E, C])).then_inc(gate_set, 1)
                pool.wait_ge(xn_set, b * 2 * TT + 2 * TT)
                pool.tensor_tensor(h[:, :, :], h[:, :, :], lnb_all[:, :].unsqueeze(1).broadcast_to([P, TT, D]),
                                   ALU.add).then_inc(hb_set, 1)

        @block.scalar
        def _(act):
            def load(dst, src, s=c_in):
                act.dma_start(dst, src).then_inc(s, 16)

            with nc.allow_non_contiguous_dma("biases by partition"):
                load(bq_sb[:, :], bq.rearrange("(k p) -> p k", p=P), bq_in)
            load(s2c_raw[:, :, :], s2c_w.rearrange("(k p) n -> p k n", p=P), raw2_in)
            for i in range(2):
                half = slice(i * C, (i + 1) * C)
                load(rw1_raw[half, :], r_w1, raw2_in)
                load(rw2_raw[half, :], r_w2, raw2_in)
                load(c2s_raw[half, :], c2s_w, raw2_in)
                load(ew1_raw[half, :, :], e_w1.rearrange("e d h -> d e h"), raw2_in)
            load(enc_raw[:, :, :], enc_w.rearrange("(k p) n -> p k n", p=P), raw2_in)
            load(dec_raw[:, :, :], dec_w.rearrange("(k p) n -> p k n", p=P), raw2_in)
            load(ew2_sb[:, :, :, :], e_w2.rearrange("e (k p) d -> p e k d", p=P))
            with nc.allow_non_contiguous_dma("biases by partition"):
                load(encb[:, :], enc_b.rearrange("(k p) -> p k", p=P))
                load(c2sb[:, :], c2s_b.rearrange("(k p) -> p k", p=P))
                load(eb1[:, :, :], e_b1.rearrange("e (k p) -> p e k", p=P))
                for i in range(2):
                    half = slice(i * C, (i + 1) * C)
                    load(s2cb[half, :], s2c_b.rearrange("(c o) -> c o", o=1))
                    load(rb1[half, :], r_b1.rearrange("(c o) -> c o", o=1))
                    load(eb2[half, :], e_b2.rearrange("(q two) d -> two d q", two=2)[i])
            for dst, src in ((decb_all, dec_b), (g_all, ln_g), (lnb_all, ln_b), (rb2_all, r_b2)):
                load(dst[:, :], src.partition_broadcast(P))
            act.wait_ge(bq_in, 16)
            with act.Fori(0, B, 1) as b:
                def std_of(n):
                    act.wait_ge(ln_var, b * 3 + n)
                    act.activation(std[:, :], mv[:, :, 1], ACT.Sqrt, bias=eps[:, 0:1]).then_inc(ln_std, 1)

                def xt_parts(n):
                    for u in range(KC * TB):
                        tb, kc = u // KC, u % KC
                        act.wait_ge(xt_mm, b * 2 * KC * TB + n * KC * TB + u + 1)
                        act.activation(xt_hi[:, kc, tb * BANK:(tb + 1) * BANK], ps[:, 2 + u, :], ACT.Copy).then_inc(xt_h, 1)

                std_of(1)
                act.activation(nrc[:, :], mv[:, :, 1], ACT.Sqrt, scale=float(D)).then_inc(n_set, 1)
                xt_parts(0)
                for u in range(2 * KC * TB):
                    kc, tb = u // TB % KC, u % TB
                    cols = slice(tb * BANK, (tb + 1) * BANK)
                    act.wait_ge(q_mm, b * 2 * KC * TB + u + 1)
                    if u < KC * TB:
                        act.activation(qt_hi[:, kc, cols], ps[:, PB[u % 4], :], ACT.Identity, bias=bq_sb[:, kc:kc + 1]).then_inc(q_h, 1)
                    else:
                        act.activation(tq_hi[:, kc, cols], ps[:, PB[u % 4], :], ACT.Copy).then_inc(q_h, 1)

                def parts_of_p(t):
                    act.wait_ge(pt_mm, b * TT + t + 1)
                    if t >= 2:
                        act.wait_ge(pv_mm, b * TT + t - 1)
                    act.activation(pt_hi[:, t % 2, :, :].rearrange("p a c -> p (a c)"),
                                   ps[:, 2 + 2 * (t % 2):4 + 2 * (t % 2), :].rearrange("p a c -> p (a c)"), ACT.Copy).then_inc(pt_h, 1)

                for t in range(TT):
                    act.wait_ge(nb_set, b * TT + t + 1)
                    if t >= 2:
                        act.wait_ge(pt_mm, b * TT + t - 1)
                    act.activation(pr[:, t % 2, :], ps[:, 0:2, :].rearrange("p a c -> p (a c)"), ACT.Exp, bias=nb[:, t:t + 1],
                                   scale=SCALE, accum_out=sums[:, t:t + 1]).then_inc(p_set, 1)
                    if t:
                        parts_of_p(t - 1)
                parts_of_p(TT - 1)
                std_of(2)
                xt_parts(1)
                act.wait_ge(c_in, 16 * CONSTS)

                def after(u, bank, func, bias):
                    act.wait_ge(f_mm, b * FU + u + 1)
                    if u >= 2:
                        act.wait_ge(f_split, b * FU + u - 1)
                    act.activation(f_sb[:, u % 2, :], ps[:, bank, :], func, bias=bias).then_inc(f_set, 1)

                for u in range(TB * MH):
                    after(u, PB[u % 4], ACT.Sigmoid, encb[:, u % MH:u % MH + 1])
                for tb in range(TB):
                    after(TB * MH + tb, 2 + tb, ACT.Identity, s2cb[:, 0:1])
                for tb in range(TB):
                    after(TB * MH + TB + tb, 4 + tb, ACT.Relu, rb1[:, 0:1])
                act.wait_ge(lg_set, b + 1)
                act.activation(small[1][:, :, :], small[0][:, :, :], ACT.Exp).then_inc(eg_set, 1)

                def hidden(n):
                    act.wait_ge(e1_mm, b * TB * E * EH + n + 1)
                    if n >= 8:
                        act.wait_ge(e2_mm, b * TB * PAIRS + (n - 8) // 4 + 1)
                    act.activation(eh[:, n % 8, :], ps[:, n % 2, :], ACT.Relu, bias=eb1[:, n // EH % E, n % EH:n % EH + 1]).then_inc(eh_set, 1)

                def gate(v):
                    act.wait_ge(cb_mm, b * TB * PAIRS + v + 1)
                    if v >= 2:
                        act.wait_ge(y_set, b * TB * PAIRS + v - 1)
                    act.activation(cb[:, v % 2, :], ps[:, 4 + v % 2, :], ACT.Copy).then_inc(cb_set, 1)

                for v in range(TB * PAIRS + 1):
                    if v < TB * PAIRS:
                        for n in range(4 * v, 4 * v + 4):
                            hidden(n)
                    if v:
                        gate(v - 1)
                for u in range(TB * MH):
                    after(TB * MH + 2 * TB + u, PB[u % 4], ACT.Sigmoid, c2sb[:, u % MH:u % MH + 1])
                for t in range(TT):
                    act.wait_ge(de_set, b * TT + t + 1)
                    act.activation(dd[:, t, :], dd[:, t, :], ACT.Sigmoid).then_inc(dd_set, 1)
                std_of(3)

        @block.vector
        def _(dve):
            dve.memset(eps[:, :], EPS)
            dve.wait_ge(raw_in, 16 * RAWS)
            dve.tensor_copy(an_hi[:, :, :], an_raw[:, :, :]).then_inc(w_hi, 1)
            dve.wait_ge(wt_mm, 2)
            turned = [(wqt_hi, wqt_lo, 0), (wvt_hi, wvt_lo, 1)]
            for hi, _lo, bank in turned:
                dve.tensor_copy(hi[:, :, :].rearrange("p k n -> p (k n)"), ps[:, bank, :]).then_inc(w_hi, 1)
            dve.wait_ge(w_hi, SPLITS)
            dve.tensor_tensor(an_lo[:, :, :], an_raw[:, :, :], an_hi[:, :, :].bitcast(F32), ALU.subtract).then_inc(w_set, 1)
            for hi, lo, bank in turned:
                dve.tensor_tensor(lo[:, :, :].rearrange("p k n -> p (k n)"), ps[:, bank, :],
                                  hi[:, :, :].rearrange("p k n -> p (k n)").bitcast(F32), ALU.subtract).then_inc(w_set, 1)
            dve.wait_ge(w_set, SPLITS)
            dve.wait_ge(id_set, 2)
            dve.wait_ge(bv_in, 16)
            with dve.Fori(0, B, 1) as b:
                chain = [0]
                CHAIN = 3 * 2 * TT + 4 + TT * 3 + TT + 37 + TB * (PAIRS + 1) + 2

                def then(ins):
                    chain[0] += 1
                    ins.then_inc(vec, 1)

                def settle():
                    dve.wait_ge(vec, b * CHAIN + chain[0])

                def step(ins):
                    then(ins)
                    settle()

                def moments(n, src, ready=None):
                    for t in range(TT):
                        if ready:
                            ready(t)
                        then(dve.bn_stats(stats[:, t, :], src[:, t, :]))
                    settle()
                    dve.sem_inc(past, 1)
                    for t in range(TT):
                        ins = dve.bn_aggr(mv[:, t, :], stats[:, t, :])
                        if t == TT - 1:
                            ins.then_inc(ln_var, 1)
                        else:
                            then(ins)
                    settle()
                    dve.wait_ge(ln_std, b * 3 + n)
                    step(dve.reciprocal(rstd[:, :], std[:, :]))

                def xt_rest(n):
                    for u in range(KC * TB):
                        tb, kc = u // KC, u % KC
                        cols = slice(tb * BANK, (tb + 1) * BANK)
                        dve.wait_ge(xt_h, b * 2 * KC * TB + n * KC * TB + u + 1)
                        dve.tensor_tensor(xt_lo[:, kc, cols], ps[:, 2 + u, :], xt_hi[:, kc, cols].bitcast(F32),
                                          ALU.subtract).then_inc(xt_l, 1)

                dve.wait_ge(h_in, b * 16 + 16)
                moments(1, h)
                dve.wait_ge(n_set, b + 1)
                step(dve.tensor_tensor(nrm[:, :], nrc[:, :], rstd[:, :], ALU.mult))
                step(dve.tensor_scalar(nrd[:, :], nrm[:, :], 1e-9, None, ALU.add))
                step(dve.reciprocal(rn[:, :], nrd[:, :]))
                step(dve.tensor_tensor(rn[:, :], rn[:, :], rstd[:, :], ALU.mult))
                for t in range(TT):
                    dve.tensor_scalar(xn[:, t, :], h[:, t, :], mv[:, t, 0:1], rn[:, t:t + 1],
                                      ALU.subtract, ALU.mult).then_inc(xn_set, 1)
                xt_rest(0)
                for u in range(2 * KC * TB):
                    kc, tb = u // TB % KC, u % TB
                    cols = slice(tb * BANK, (tb + 1) * BANK)
                    dve.wait_ge(q_h, b * 2 * KC * TB + u + 1)
                    if u < KC * TB:
                        dve.scalar_tensor_tensor(out=qt_lo[:, kc, cols], in0=ps[:, PB[u % 4], :], scalar=bq_sb[:, kc:kc + 1],
                                                 in1=qt_hi[:, kc, cols].bitcast(F32), op0=ALU.add, op1=ALU.subtract).then_inc(q_l, 1)
                    else:
                        dve.tensor_tensor(tq_lo[:, kc, cols], ps[:, PB[u % 4], :], tq_hi[:, kc, cols].bitcast(F32),
                                          ALU.subtract).then_inc(q_l, 1)
                for t in range(TT):
                    dve.wait_ge(v_mm, b * TT + t + 1)
                    dve.tensor_tensor(v_f[:, t, :], ps[:, 2 + t % 4, 0:D], bv_all[:, :], ALU.add).then_inc(v_set, 1)
                dve.wait_ge(v_set, b * TT + TT)
                dve.tensor_copy(v_hi[:, :, :], v_f[:, :, :]).then_inc(v_parts, 1)
                dve.wait_ge(v_parts, b * 2 + 1)
                dve.tensor_tensor(v_lo[:, :, :], v_f[:, :, :], v_hi[:, :, :].bitcast(F32), ALU.subtract).then_inc(v_parts, 1)

                def rest_of_p(t):
                    dve.wait_ge(pt_h, b * TT + t + 1)
                    dve.tensor_tensor(pt_lo[:, t % 2, :, :].rearrange("p a c -> p (a c)"),
                                      ps[:, 2 + 2 * (t % 2):4 + 2 * (t % 2), :].rearrange("p a c -> p (a c)"),
                                      pt_hi[:, t % 2, :, :].rearrange("p a c -> p (a c)").bitcast(F32), ALU.subtract).then_inc(pt_l, 1)

                def context(t):
                    step(dve.reciprocal(rsum[:, t:t + 1], sums[:, t:t + 1]))
                    step(dve.tensor_tensor(cf[:, t:t + 1], rsum[:, t:t + 1], nrm[:, t:t + 1], ALU.mult))
                    dve.wait_ge(pv_mm, b * TT + t + 1)
                    dve.scalar_tensor_tensor(out=h[:, t, :], in0=ps[:, 6 + t % 2, 0:D], scalar=cf[:, t:t + 1],
                                             in1=h[:, t, :], op0=ALU.mult, op1=ALU.add).then_inc(h_set, 1)

                for t in range(TT):
                    dve.wait_ge(s_mm, b * TT + t + 1)
                    step(dve.tensor_reduce(smax[:, t:t + 1], ps[:, 0:2, :], AX.XY, ALU.max))
                    dve.tensor_scalar(nb[:, t:t + 1], smax[:, t:t + 1], -SCALE, None, ALU.mult).then_inc(nb_set, 1)
                    if t:
                        rest_of_p(t - 1)
                    if t >= 2:
                        context(t - 2)
                rest_of_p(TT - 1)
                context(TT - 2)
                context(TT - 1)
                dve.wait_ge(h_set, b * TT + TT)
                moments(2, h)
                for t in range(TT):
                    dve.tensor_scalar(xn[:, t, :], h[:, t, :], mv[:, t, 0:1], rstd[:, t:t + 1],
                                      ALU.subtract, ALU.mult).then_inc(xn_set, 1)
                xt_rest(1)
                dve.wait_ge(c_in, 16 * CONSTS)

                def parts(u, hi, lo):
                    dve.wait_ge(f_set, b * FU + u + 1)
                    step(dve.tensor_copy(hi, f_sb[:, u % 2, :]))
                    dve.tensor_tensor(lo, f_sb[:, u % 2, :], hi.bitcast(F32), ALU.subtract).then_inc(f_split, 1)

                def stacked(u, dst):
                    dve.wait_ge(f_set, b * FU + u + 1)
                    then(dve.tensor_copy(dst[0:C, :], f_sb[0:C, u % 2, :]))
                    step(dve.tensor_copy(ch[C:P, :], f_sb[C:P, u % 2, :]))
                    dve.tensor_tensor(dst[C:P, :], f_sb[C:P, u % 2, :], ch[C:P, :].bitcast(F32), ALU.subtract).then_inc(f_split, 1)

                for u in range(TB * MH):
                    tb, m = u // MH, u % MH
                    cols = slice(tb * BANK, (tb + 1) * BANK)
                    parts(u, sp_hi[:, m, cols], sp_lo[:, m, cols])
                for tb in range(TB):
                    dve.wait_ge(f_split, b * FU + TB * MH + tb)
                    stacked(TB * MH + tb, cs[:, tb * BANK:(tb + 1) * BANK])
                for tb in range(TB):
                    dve.wait_ge(f_split, b * FU + TB * MH + TB + tb)
                    stacked(TB * MH + TB + tb, rs[:, tb * BANK:(tb + 1) * BANK])
                lg, eg, one, two, tmp, comb = (s[:, :, :] for s in small)
                m1, r1, m2, r2, den = (s[:, :] for s in tiny)

                def wide(s):
                    return s.unsqueeze(2).broadcast_to([P, TT, E])

                order = desc[:, :].unsqueeze(1).broadcast_to([P, TT, E])
                dve.wait_ge(lg_mm, b + 1)
                step(dve.tensor_tensor(tmp, ps[:, 2, 0:TT * E].rearrange("p (t e) -> p t e", e=E),
                                       rb2_all[:, :].unsqueeze(1).broadcast_to([P, TT, E]), ALU.add))
                step(dve.tensor_reduce(m1, tmp, AX.X, ALU.max))
                dve.tensor_tensor(lg, tmp, wide(m1), ALU.subtract).then_inc(lg_set, 1)
                dve.wait_ge(eg_set, b + 1)
                step(dve.tensor_reduce(m1, eg, AX.X, ALU.max))
                step(dve.tensor_tensor(tmp, eg, wide(m1), ALU.is_equal))
                step(dve.tensor_tensor(tmp, tmp, order, ALU.mult))
                step(dve.tensor_reduce(r1, tmp, AX.X, ALU.max))
                step(dve.tensor_tensor(one, order, wide(r1), ALU.is_equal))
                step(dve.scalar_tensor_tensor(out=two, in0=one, scalar=-2.0, in1=eg, op0=ALU.mult, op1=ALU.add))
                step(dve.tensor_reduce(m2, two, AX.X, ALU.max))
                step(dve.tensor_tensor(tmp, two, wide(m2), ALU.is_equal))
                step(dve.tensor_tensor(tmp, tmp, order, ALU.mult))
                step(dve.tensor_reduce(r2, tmp, AX.X, ALU.max))
                step(dve.tensor_tensor(two, order, wide(r2), ALU.is_equal))
                step(dve.tensor_tensor(one, one, two, ALU.add))
                step(dve.tensor_tensor(one, one, eg, ALU.mult))
                step(dve.tensor_tensor(den, m1, m2, ALU.add))
                step(dve.reciprocal(r1, den))
                dve.tensor_tensor(comb, one, wide(r1), ALU.mult).then_inc(comb_set, 1)
                for v in range(TB * PAIRS):
                    tb, q = v // PAIRS, v % PAIRS
                    dve.wait_ge(e2_mm, b * TB * PAIRS + v + 1)
                    dve.wait_ge(cb_set, b * TB * PAIRS + v + 1)
                    if q:
                        settle()
                        dve.scalar_tensor_tensor(out=y[:, :], in0=ps[:, 6 + v % 2, :], scalar=eb2[:, q:q + 1], in1=cb[:, v % 2, :],
                                                 op0=ALU.add, op1=ALU.mult).then_inc(y_set, 1)
                        dve.wait_ge(y_set, b * TB * PAIRS + v + 1)
                        then(dve.tensor_tensor(ysum[:, tb, :], ysum[:, tb, :], y[:, :], ALU.add))
                    else:
                        dve.scalar_tensor_tensor(out=ysum[:, tb, :], in0=ps[:, 6 + v % 2, :], scalar=eb2[:, q:q + 1],
                                                 in1=cb[:, v % 2, :], op0=ALU.add, op1=ALU.mult).then_inc(y_set, 1)
                        dve.wait_ge(y_set, b * TB * PAIRS + v + 1)
                    if q == PAIRS - 1:
                        settle()
                        cols = slice(tb * BANK, (tb + 1) * BANK)
                        step(dve.tensor_copy(ys_hi[:, cols], ysum[:, tb, :]))
                        dve.tensor_tensor(ys_lo[:, cols], ysum[:, tb, :], ys_hi[:, cols].bitcast(F32), ALU.subtract).then_inc(ys_set, 1)
                for u in range(TB * MH):
                    tb, m = u // MH, u % MH
                    cols = slice(tb * BANK, (tb + 1) * BANK)
                    parts(TB * MH + 2 * TB + u, rt_hi[:, m, cols], rt_lo[:, m, cols])
                for t in range(TT):
                    dve.wait_ge(de_mm, b * TT + t + 1)
                    dve.tensor_tensor(dd[:, t, :], ps[:, 2 + t % 4, 0:D], decb_all[:, :], ALU.add).then_inc(de_set, 1)
                moments(3, dd, lambda t: dve.wait_ge(dd_set, b * TT + t + 1))
                for t in range(TT):
                    then(dve.scalar_tensor_tensor(out=dd[:, t, :], in0=dd[:, t, :], scalar=mv[:, t, 0:1], in1=g_all[:, :],
                                                  op0=ALU.subtract, op1=ALU.mult))
                settle()
                dve.wait_ge(hb_set, b + 1)
                for t in range(TT):
                    dve.scalar_tensor_tensor(out=h[:, t, :], in0=dd[:, t, :], scalar=rstd[:, t:t + 1], in1=h[:, t, :],
                                             op0=ALU.mult, op1=ALU.add).then_inc(out_set, 1)
                assert chain[0] == CHAIN, (chain[0], CHAIN)

        @block.tensor
        def _(pe):
            pe.wait_ge(id_set, 1)
            pe.wait_ge(raw_in, 16 * RAWS)
            for bank, raw in enumerate((wq_raw, wv_raw)):
                for oc in range(KC):
                    for hc in range(KC):
                        ins = pe.transpose(ps[:, bank, hc * D + oc * P:hc * D + (oc + 1) * P], raw[:, oc, hc * P:(hc + 1) * P],
                                           ident[:, :])
                ins.then_inc(wt_mm, 1)
            pe.wait_ge(w_set, SPLITS)
            with pe.Fori(0, B, 1) as b:
                def transposes(n):
                    for tb in range(TB):
                        for kc in range(KC):
                            for i in range(4):
                                t = 4 * tb + i
                                if kc == 0:
                                    pe.wait_ge(xn_set, b * 2 * TT + n * TT + t + 1)
                                ins = pe.transpose(ps[:, 2 + KC * tb + kc, i * P:(i + 1) * P], xn[:, t, kc * P:(kc + 1) * P],
                                                   ident[:, :])
                            ins.then_inc(xt_mm, 1)

                def product(dst, pairs):
                    for i, (w, a) in enumerate(pairs):
                        ins = pe.matmul(dst, w, a, start=(i == 0), stop=(i == len(pairs) - 1))
                    return ins

                def three(hi_a, lo_a, hi_b, lo_b):
                    return [(hi_a, hi_b), (hi_a, lo_b), (lo_a, hi_b)]

                transposes(0)
                for u in range(2 * KC * TB):
                    kc, tb = u // TB % KC, u % TB
                    cols = slice(tb * BANK, (tb + 1) * BANK)
                    mc = slice(kc * P, (kc + 1) * P)
                    if u < TB:
                        pe.wait_ge(xt_l, b * 2 * KC * TB + KC * (tb + 1))
                    if u >= 4:
                        pe.wait_ge(q_l, b * 2 * KC * TB + (KC * TB if u == KC * TB else u - 3))
                    w_h, w_l, a_h, a_l = (wqt_hi, wqt_lo, xt_hi, xt_lo) if u < KC * TB else (an_hi, an_lo, qt_hi, qt_lo)
                    product(ps[:, PB[u % 4], :], [z for c in range(KC) for z in three(w_h[:, c, mc], w_l[:, c, mc], a_h[:, c, cols],
                                                                                      a_l[:, c, cols])]).then_inc(q_mm, 1)
                for t in range(TT):
                    rows = slice(t * P, (t + 1) * P)
                    if t >= 4:
                        pe.wait_ge(v_set, b * TT + t - 3)
                    product(ps[:, 2 + t % 4, 0:D], [z for c in range(KC) for z in three(xt_hi[:, c, rows], xt_lo[:, c, rows],
                                                                                        wvt_hi[:, c, :], wvt_lo[:, c, :])]).then_inc(v_mm, 1)
                pe.wait_ge(q_l, b * 2 * KC * TB + 2 * KC * TB)
                pe.wait_ge(v_parts, b * 2 + 2)

                def values(t):
                    pe.wait_ge(pt_l, b * TT + t + 1)
                    if t >= 2:
                        pe.wait_ge(h_set, b * TT + t - 1)
                    product(ps[:, 6 + t % 2, 0:D], [z for c in range(TT) for z in three(
                        pt_hi[:, t % 2, c, :], pt_lo[:, t % 2, c, :], v_hi[:, c, :], v_lo[:, c, :])]).then_inc(pv_mm, 1)

                def turn(t):
                    pe.wait_ge(p_set, b * TT + t + 1)
                    if t >= 2:
                        pe.wait_ge(pt_l, b * TT + t - 1)
                    for c in range(TT):
                        bank = 2 + 2 * (t % 2) + c // 4
                        ins = pe.transpose(ps[:, bank, c % 4 * P:(c % 4 + 1) * P], pr[:, t % 2, c * P:(c + 1) * P], ident[:, :])
                    ins.then_inc(pt_mm, 1)

                for t in range(TT + 2):
                    if t < TT:
                        rows = slice(t * P, (t + 1) * P)
                        if t:
                            pe.wait_ge(p_set, b * TT + t)
                        for kh in range(2):
                            keys = slice(kh * BANK, (kh + 1) * BANK)
                            ins = product(ps[:, kh, :], [z for c in range(KC) for z in three(
                                qt_hi[:, c, rows], qt_lo[:, c, rows], tq_hi[:, c, keys], tq_lo[:, c, keys])])
                        ins.then_inc(s_mm, 1)
                    if 1 <= t <= TT:
                        turn(t - 1)
                    if t >= 2:
                        values(t - 2)
                transposes(1)
                pe.wait_ge(f_lo, SPLITS2)
                pe.wait_ge(c_in, 16 * CONSTS)
                for u in range(TB * MH):
                    tb, m = u // MH, u % MH
                    cols = slice(tb * BANK, (tb + 1) * BANK)
                    mc = slice(m * P, (m + 1) * P)
                    if m == 0:
                        pe.wait_ge(xt_l, b * 2 * KC * TB + KC * TB + KC * (tb + 1))
                    if u >= 4:
                        pe.wait_ge(f_set, b * FU + u - 3)
                    product(ps[:, PB[u % 4], :], [z for c in range(KC) for z in three(
                        enc_hi[:, c, mc], enc_lo[:, c, mc], xt_hi[:, c, cols], xt_lo[:, c, cols])]).then_inc(f_mm, 1)
                for tb in range(TB):
                    cols = slice(tb * BANK, (tb + 1) * BANK)
                    pe.wait_ge(f_split, b * FU + MH * (tb + 1))
                    product(ps[:, 2 + tb, :], [z for m in range(MH) for z in three(
                        s2c_hi[:, m, :, :].rearrange("p a c -> p (a c)"), s2c_lo[:, m, :, :].rearrange("p a c -> p (a c)"),
                        sp_hi[:, m, cols], sp_lo[:, m, cols])]).then_inc(f_mm, 1)
                for tb in range(TB):
                    cols = slice(tb * BANK, (tb + 1) * BANK)
                    pe.wait_ge(f_split, b * FU + TB * MH + tb + 1)
                    product(ps[:, 4 + tb, :], [(w[:, :, :].rearrange("p a c -> p (a c)"), cs[:, cols])
                                               for w in (rw1_hi, rw1_lo)]).then_inc(f_mm, 1)
                for t in range(TT):
                    if t % 4 == 0:
                        pe.wait_ge(f_split, b * FU + TB * MH + TB + t // 4 + 1)
                    ins = product(ps[:, 2, t * E:(t + 1) * E], [(rs[:, t * P:(t + 1) * P], w[:, :]) for w in (rw2_hi, rw2_lo)])
                ins.then_inc(lg_mm, 1)

                def experts_in(v):
                    for n in range(4 * v, 4 * v + 4):
                        tb, e, hh = n // (E * EH), n // EH % E, n % EH
                        if n >= 2:
                            pe.wait_ge(eh_set, b * TB * E * EH + n - 1)
                        product(ps[:, n % 2, :], [(w[:, e, hh * P:(hh + 1) * P], cs[:, tb * BANK:(tb + 1) * BANK])
                                                  for w in (ew1_hi, ew1_lo)]).then_inc(e1_mm, 1)

                def gates(v):
                    tb, q = v // PAIRS, v % PAIRS
                    if v >= 2:
                        pe.wait_ge(cb_set, b * TB * PAIRS + v - 1)
                    if q == 0:
                        pe.wait_ge(gate_set, b * TB + tb + 1)
                    for i in range(4):
                        ins = pe.transpose(ps[:, 4 + v % 2, i * P:(i + 1) * P],
                                           gate_w[:, 4 * tb + i, 2 * q:2 * q + 2, :].rearrange("p a c -> p (a c)"), ident[:, :])
                    ins.then_inc(cb_mm, 1)

                def experts_out(v):
                    q = v % PAIRS
                    pe.wait_ge(eh_set, b * TB * E * EH + 4 * v + 4)
                    if v >= 2:
                        pe.wait_ge(y_set, b * TB * PAIRS + v - 1)
                    for hh in range(EH):
                        for i in range(2):
                            ins = pe.matmul(ps[C * i:C * i + C, 6 + v % 2, :], ew2_sb[:, 2 * q + i, hh, :],
                                            eh[:, (4 * v + 2 * i + hh) % 8, :], start=(hh == 0), stop=(hh == EH - 1))
                    ins.then_inc(e2_mm, 1)

                experts_in(0)
                experts_in(1)
                for v in range(TB * PAIRS):
                    gates(v)
                    experts_out(v)
                    if v + 2 < TB * PAIRS:
                        experts_in(v + 2)
                for u in range(TB * MH):
                    tb, m = u // MH, u % MH
                    cols = slice(tb * BANK, (tb + 1) * BANK)
                    mc = slice(m * P, (m + 1) * P)
                    if m == 0:
                        pe.wait_ge(ys_set, b * TB + tb + 1)
                    if u == 0:
                        pe.wait_ge(y_set, b * TB * PAIRS + TB * PAIRS)
                    if u >= 4:
                        pe.wait_ge(f_set, b * FU + TB * MH + 2 * TB + u - 3)
                    product(ps[:, PB[u % 4], :], three(c2s_hi[:, mc], c2s_lo[:, mc], ys_hi[:, cols], ys_lo[:, cols])).then_inc(f_mm, 1)
                for t in range(TT):
                    rows = slice(t * P, (t + 1) * P)
                    if t % 4 == 0:
                        pe.wait_ge(f_split, b * FU + TB * MH + 2 * TB + MH * (t // 4 + 1))
                    if t >= 4:
                        pe.wait_ge(de_set, b * TT + t - 3)
                    product(ps[:, 2 + t % 4, 0:D], [z for m in range(MH) for z in three(
                        rt_hi[:, m, rows], rt_lo[:, m, rows], dec_hi[:, m, :], dec_lo[:, m, :])]).then_inc(de_mm, 1)

def two_layers(nc, x, tok_w, *rest):
    layer0, layer1, out = rest[:8], rest[8:-1], rest[-1]
    h_mid = nc.dram_tensor("h_mid", [x.shape[0], x.shape[1], tok_w.shape[1]], F32, kind="Internal").ap()
    first_layer(nc, x, tok_w, *layer0, h_mid)
    second_layer(nc, h_mid, *layer1, out)


_INS = [
    'x', 'L0_tok_W', 'L0_attn_qkv_w', 'L0_attn_qkv_b', 'L0_attn_proj_w', 'L0_attn_proj_b', 'L0_ffn_w1',
    'L0_ffn_b1', 'L0_ffn_w2', 'L0_ffn_b2', 'L1_attn_Wq', 'L1_attn_bq', 'L1_attn_Wv', 'L1_attn_bv',
    'L1_attn_anomaly_matrix', 'L1_ffn_enc_w', 'L1_ffn_enc_b', 'L1_ffn_s2c_w', 'L1_ffn_s2c_b', 'L1_ffn_r_w1',
    'L1_ffn_r_b1', 'L1_ffn_r_w2', 'L1_ffn_r_b2', 'L1_ffn_e_w1', 'L1_ffn_e_b1', 'L1_ffn_e_w2', 'L1_ffn_e_b2',
    'L1_ffn_c2s_w', 'L1_ffn_c2s_b', 'L1_ffn_dec_w', 'L1_ffn_dec_b', 'L1_ffn_ln_g', 'L1_ffn_ln_b',
]


def kernel(**inputs):
    import numpy as _np
    import concourse.bacc as _bacc
    from concourse import mybir as _mybir
    from concourse.bass_utils import run_bass_kernel_spmd as _run

    nc = _bacc.Bacc("TRN2", target_bir_lowering=False, num_devices=1)
    arrays, args = {}, []
    for name in _INS:
        a = _np.ascontiguousarray(inputs[name])
        arrays[f"in_{name}_dram"] = a
        args.append(nc.dram_tensor(f"in_{name}_dram", a.shape, _mybir.dt.from_np(a.dtype), kind="ExternalInput").ap())
    shape = [*inputs["x"].shape, inputs["L0_tok_W"].shape[1]]
    args.append(nc.dram_tensor("out_dram", shape, _mybir.dt.float32, kind="ExternalOutput").ap())
    two_layers(nc, *args)
    r = _run(nc, [arrays], core_ids=[0])
    return r.results[0]["out_dram"]
```

```python
from contextlib import ExitStack

import concourse.bass as bass
from concourse import mybir

F32 = mybir.dt.float32
F32R = mybir.dt.float32r
I32 = mybir.dt.int32
ALU = mybir.AluOpType
ACT = mybir.ActivationFunctionType
AX = mybir.AxisListType

P = 128
BANK = 512
EARLY_AT = 223200


def first_layer(nc, x, tok_w, qkv_w, qkv_b, proj_w, proj_b, w1, b1, w2, b2, h_mid, early_loads, early_in):
    B, N = x.shape
    D = tok_w.shape[1]
    KC = D // P
    TT = N // P
    TB = N // BANK
    HEADS, GH = 16, 4
    HD = D // HEADS
    G = HEADS // GH
    WIDTH = w1.shape[1]
    M1 = WIDTH // P
    SCALE = float(HD) ** -0.5
    EPS = 1e-5
    SLOTS = 10
    KR = 128
    NEG = 4 * HD
    VC = HD + 1
    STEPS = TB * TT
    UNITS = GH * TT * 2
    US = 4
    AHEAD = UNITS + 12

    def units_before(n):
        return min(AHEAD + US * n, G * UNITS)

    MAXED = [None] + [min(n for n in range(G * STEPS) if units_before(n) >= (g + 1) * UNITS) for g in range(1, G)]
    RING = 6
    FIRST = 8
    SIDES = G * TB - FIRST + TT
    LATE = 3
    ctx = ExitStack()
    with ctx:
        base = (nc.sbuf_base + 31) // 32 * 32
        top = [base]

        def at(name, shape, dt, offset=None):
            size = 4
            for n in shape[1:]:
                size *= n
            if offset is None:
                offset = top[0]
                top[0] += (size + 31) // 32 * 32
            return nc.alloc_sbuf_tensor_at(name, shape, dt, offset=offset)

        h = at("h", [P, TT, D], F32)
        xn_at = top[0]
        xn = at("xn", [P, TT, D], F32)
        xt_at = top[0]
        xt_hi = at("xt_hi", [P, KC, N], F32R)
        xt_lo = at("xt_lo", [P, KC, N], F32R)
        w1_raw = at("w1_raw", [P, KC, WIDTH], F32, xt_at)
        w2_raw = at("w2_raw", [P, M1, D], F32, xt_at + 4 * KC * WIDTH)
        qk_at = top[0]
        qk_hi = at("qk_hi", [P, G, N], F32R)
        qk_lo = at("qk_lo", [P, G, N], F32R)
        w1_hi = at("w1_hi", [P, KC, WIDTH], F32R, qk_at)
        w1_lo = at("w1_lo", [P, KC, WIDTH], F32R, qk_at + 4 * KC * WIDTH)
        w2_hi = at("w2_hi", [P, M1, D], F32R, qk_at + 8 * KC * WIDTH)
        w2_lo = at("w2_lo", [P, M1, D], F32R, qk_at + 8 * KC * WIDTH + 4 * M1 * D)
        v_sb = at("v_sb", [P, TT, HEADS, 2 * HD], F32)
        stack_at = top[0]
        k_stack = at("k_stack", [P, SLOTS, N], F32R)
        q_stack = at("q_stack", [P, SLOTS, N], F32R)
        hid_hi = at("hid_hi", [P, M1, N], F32R, stack_at)
        hid_lo = at("hid_lo", [P, M1, N], F32R, stack_at + 4 * M1 * N)
        p_at = top[0]
        p_sb = at("p_sb", [P, 2, GH, BANK], F32)
        qkv_raw = at("qkv_raw", [P, KC, 3 * D], F32, p_at)
        proj_raw = at("proj_raw", [P, KC, D], F32, p_at + 12 * KC * D)
        hid_f = at("hid_f", [P, 2, BANK], F32, p_at)
        ot_sb = at("ot_sb", [P, 2, BANK], F32)
        wqk_hi = at("wqk_hi", [P, KC, G, P], F32R)
        wqk_lo = at("wqk_lo", [P, KC, G, P], F32R)
        wv_hi = at("wv_hi", [P, KC, D], F32R)
        wv_lo = at("wv_lo", [P, KC, D], F32R)
        wp_hi = at("wp_hi", [P, KC, D], F32R)
        wp_lo = at("wp_lo", [P, KC, D], F32R)
        ident = at("ident", [P, P], F32)
        bv_all = at("bv_all", [P, D], F32)
        bp_all = at("bp_all", [P, D], F32)
        b2_all = at("b2_all", [P, D], F32)
        qk_b = at("qk_b", [P, G], F32)
        b1_sb = at("b1_sb", [P, M1], F32)
        idx = at("idx", [P, TT], I32)
        idx_all = at("idx_all", [P, B + 1, TT], I32)
        stats = at("stats", [P, TT, 6], F32)
        mv = at("mv", [P, TT, 2], F32)
        rstd = at("rstd", [P, TT], F32)
        std = at("std", [P, TT], F32)
        eps = at("eps", [P, 1], F32)
        mx = at("mx", [P, 2, UNITS], F32)
        mq = at("mq", [P, GH * TT], F32)
        nm_hi = at("nm_hi", [GH * TT, P], F32R)
        nm_lo = at("nm_lo", [GH * TT, P], F32R)
        rs = at("rs", [P, 4, GH], F32)
        assert top[0] <= EARLY_AT, top[0]
        ps = ctx.enter_context(nc.psum_tensor("ps", [P, 8, BANK], F32))

        def sem(name):
            return ctx.enter_context(nc.semaphore(name))

        w_in = sem("w_in")
        c_in = sem("c_in")
        ones_set = sem("ones_set")
        id_set = sem("id_set")
        w_split = sem("w_split")
        v_ones = sem("v_ones")
        idx_in = sem("idx_in")
        all_in = sem("all_in")
        h_set = sem("h_set")
        got = [sem(f"got{t}") for t in range(TT)]
        past = sem("past")
        vec = sem("vec")
        ln_var = sem("ln_var")
        ln_std = sem("ln_std")
        xn_set = sem("xn_set")
        xt_mm = sem("xt_mm")
        xt_h = sem("xt_h")
        xt_l = sem("xt_l")
        qk_mm = sem("qk_mm")
        qk_h = sem("qk_h")
        qk_l = sem("qk_l")
        v_mm = sem("v_mm")
        v_out = sem("v_out")
        v_set = sem("v_set")
        rows_set = sem("rows_set")
        slot_in = [sem(f"slot_in{s}") for s in range(SLOTS)]
        w12_in = sem("w12_in")
        w12_split = sem("w12_split")
        s_mm = sem("s_mm")
        s_max = sem("s_max")
        m_set = sem("m_set")
        m_tr = sem("m_tr")
        nm_set = sem("nm_set")
        nm_in = sem("nm_in")
        st_mm = sem("st_mm")
        p_set = sem("p_set")
        pv_mm = sem("pv_mm")
        ot_set = sem("ot_set")
        ot_tr = sem("ot_tr")
        o_norm = sem("o_norm")
        hb_set = sem("hb_set")
        pr_mm = sem("pr_mm")
        h1_set = sem("h1_set")
        w1_mm = sem("w1_mm")
        hid_set = sem("hid_set")
        hid_split = sem("hid_split")
        w2_mm = sem("w2_mm")
        h2_set = sem("h2_set")
        mid_out = sem("mid_out")
        HIW = 8 * HD

        PB = (0, 1, 6, 7)
        XT_N = 3 * 2 * TB

        block = ctx.enter_context(nc.Block())

        def wqkv_cols(t, part):
            return t[:, :, :, part * GH * HD:(part + 1) * GH * HD]

        @block.sync
        def _(sp):
            sp.dma_start(idx[:, :], x[0:1, :].rearrange("o (p t) -> p (o t)", p=P)).then_inc(idx_in, 16)
            sp.dma_start(qkv_raw[:, :, :], qkv_w.rearrange("(k p) n -> p k n", p=P)).then_inc(w_in, 16)
            sp.dma_start(proj_raw[:, :, :], proj_w.rearrange("(k p) n -> p k n", p=P)).then_inc(w_in, 16)
            with nc.allow_non_contiguous_dma("biases by partition"):
                for part in range(2):
                    sp.dma_start(qk_b[part * 64:part * 64 + 64, :],
                                 qkv_b[part * D:(part + 1) * D].rearrange("(g c) -> c g", g=G)).then_inc(c_in, 16)
                sp.dma_start(b1_sb[:, :], b1.rearrange("(m p) -> p m", p=P)).then_inc(c_in, 16)
            sp.dma_start(bv_all[:, :], qkv_b[2 * D:3 * D].partition_broadcast(P)).then_inc(c_in, 16)
            sp.dma_start(bp_all[:, :], proj_b.partition_broadcast(P)).then_inc(c_in, 16)
            sp.dma_start(b2_all[:, :], b2.partition_broadcast(P)).then_inc(c_in, 16)
            sp.sem_inc(mid_out, 16)
            with nc.allow_non_contiguous_dma("token numbers"):
                sp.dma_start(idx_all[:, 0:B, :], x.rearrange("b (p t) -> p b t", p=P)).then_inc(all_in, 16)
            for dst, src in early_loads:
                sp.dma_start(dst, src).then_inc(early_in, 16)
            sp.wait_ge(all_in, 16)
            sp.wait_ge(id_set, 2)
            with sp.Fori(0, B, 1) as b:
                for t in range(TT):
                    sp.wait_ge(got[t], b * 16 + 16)
                sp.dma_start(idx[:, :], idx_all[:, bass.ds(b + 1, 1), :].rearrange("p o t -> p (o t)")).then_inc(idx_in, 16)

                def load_stacks(hd):
                    g, j, slot = hd // GH, hd % GH, hd % SLOTS
                    if hd < SLOTS:
                        sp.wait_ge(qk_l, b * G * TB + TB * (g + 1))
                    else:
                        sp.wait_ge(st_mm, b * G * 2 * STEPS + 2 * STEPS * ((hd - SLOTS) // GH + 1))
                        sp.wait_ge(pv_mm, b * G * STEPS + 1)
                    q = slice(j * HD, (j + 1) * HD)
                    k = slice(64 + j * HD, 64 + (j + 1) * HD)
                    for r, (qp, kp) in enumerate(((qk_hi, qk_hi), (qk_hi, qk_lo), (qk_lo, qk_hi), (qk_lo, qk_lo))):
                        sp.dma_start(q_stack[r * HD:(r + 1) * HD, slot, :].bitcast(F32), qp[q, g, :].bitcast(F32)).then_inc(slot_in[slot], 16)
                        sp.dma_start(k_stack[r * HD:(r + 1) * HD, slot, :].bitcast(F32), kp[k, g, :].bitcast(F32)).then_inc(slot_in[slot], 16)

                def load_neg_max(g):
                    sp.wait_ge(nm_set, b * 2 * G + 2 * g + 2)
                    s0 = g * GH % SLOTS
                    first = min(GH, SLOTS - s0)
                    for row, src in ((NEG, nm_hi), (NEG + 1, nm_lo)):
                        for lo, n, slot in ((0, first, s0), (first, GH - first, 0)):
                            if n:
                                sp.dma_start(
                                    q_stack[row:row + 1, slot:slot + n, :].bitcast(F32).rearrange("o s (t c) -> o (s t) c", c=P),
                                    src[lo * TT:(lo + n) * TT, :].bitcast(F32),
                                ).then_inc(nm_in, 16)

                for hd in range(SLOTS):
                    if hd == 2 * GH:
                        load_neg_max(0)
                    load_stacks(hd)
                sp.wait_ge(v_mm, b * TT + TT)
                sp.dma_start(w1_raw[:, :, :], w1.rearrange("(k p) n -> p k n", p=P)).then_inc(w12_in, 16)
                sp.dma_start(w2_raw[:, :, :], w2.rearrange("(m p) n -> p m n", p=P)).then_inc(w12_in, 16)
                load_neg_max(1)
                for hd in range(SLOTS, 3 * GH + 2):
                    load_stacks(hd)
                load_neg_max(2)
                for hd in range(3 * GH + 2, HEADS):
                    load_stacks(hd)
                load_neg_max(3)
                sp.wait_ge(h2_set, b * TT + TT)
                sp.dma_start(h_mid[bass.ds(b, 1)].rearrange("o (p t) d -> p (o t) d", p=P), h[:, :, :]).then_inc(mid_out, 16)
            sp.wait_ge(mid_out, 16 * B + 16)

        NMD = [2 * 16 * (2 if (g * GH % SLOTS) + GH > SLOTS else 1) for g in range(G)]
        NMC = [sum(NMD[:g + 1]) for g in range(G)]

        @block.gpsimd
        def _(pool):
            pool.memset(ident[:, :], 0.0).then_inc(ones_set, 1)
            pool.wait_ge(ones_set, 1)
            pool.affine_select(out=ident[:, :], in_=ident[:, :], compare_op=ALU.not_equal, fill=1.0, base=0,
                               pattern=[[-1, P]], channel_multiplier=1).then_inc(id_set, 1)
            pool.memset(v_sb[:, :, :, HD:2 * HD], 0.0).then_inc(v_ones, 1)
            pool.wait_ge(v_ones, 1)
            pool.memset(v_sb[:, :, :, HD:HD + 1], 1.0).then_inc(v_ones, 1)
            pool.memset(idx_all[:, B:B + 1, :], 0).then_inc(id_set, 1)

            def gather():
                for t in range(TT):
                    pool.indirect_dma_start(out=xn[:, t, :], out_offset=None, in_=tok_w,
                                            in_offset=bass.IndirectOffsetOnAxis(ap=idx[:, t:t + 1], axis=0)
                                            ).then_inc(got[t], 16)

            pool.wait_ge(id_set, 2)
            pool.wait_ge(idx_in, 16)
            gather()
            with pool.Fori(0, B, 1) as b:
                pool.wait_ge(mid_out, b * 16 + 16)
                pool.wait_ge(v_ones, 2)
                for n, (s0, s1) in enumerate(((0, GH), (GH, SLOTS))):
                    pool.sem_inc(past, 1)
                    pool.memset(q_stack[NEG:KR, s0:s1, :].bitcast(I32), 0).then_inc(rows_set, 1)
                    pool.wait_ge(rows_set, b * 6 + 2 * n + 1)
                    pool.sem_inc(past, 1)
                    pool.memset(k_stack[NEG:KR, s0:s1, :].bitcast(F32), 1.0).then_inc(rows_set, 1)
                    pool.wait_ge(rows_set, b * 6 + 2 * n + 2)
                pool.wait_ge(c_in, 16 * 6)
                pool.wait_ge(v_out, b * TT + TT)
                for half in range(2):
                    tiles = slice(half * TT // 2, (half + 1) * TT // 2)
                    values = v_sb[:, tiles, :, 0:HD]
                    bias = bv_all[:, :].rearrange("p (a c) -> p a c", c=HD).unsqueeze(1).broadcast_to([P, TT // 2, HEADS, HD])
                    pool.tensor_tensor(values, values, bias, ALU.add).then_inc(v_set, 1)
                pool.wait_ge(h_set, b * TT + TT)
                pool.wait_ge(c_in, 16 * 6)
                pool.tensor_tensor(h[:, :, :], h[:, :, :], bp_all[:, :].unsqueeze(1).broadcast_to([P, TT, D]),
                                   ALU.add).then_inc(hb_set, 1)
                pool.wait_ge(st_mm, b * G * 2 * STEPS + 2 * STEPS)
                pool.wait_ge(hb_set, b * 2 + 1)
                pool.sem_inc(past, 1)
                pool.memset(q_stack[NEG:NEG + 2, 0:GH, :].bitcast(F32), 0.0).then_inc(rows_set, 1)
                pool.wait_ge(rows_set, b * 6 + 5)
                pool.wait_ge(st_mm, b * G * 2 * STEPS + 4 * STEPS)
                pool.sem_inc(past, 1)
                pool.memset(q_stack[NEG:NEG + 2, GH:HEADS - SLOTS, :].bitcast(F32), 0.0).then_inc(rows_set, 1)
                pool.wait_ge(w12_in, b * 32 + 32)
                for s in range(SLOTS):
                    uses = 2 if s < HEADS - SLOTS else 1
                    pool.wait_ge(slot_in[s], b * uses * HIW + uses * HIW)
                pool.wait_ge(rows_set, b * 6 + 6)
                pool.sem_inc(past, 1)
                pool.tensor_copy(w1_hi[:, :, :], w1_raw[:, :, :]).then_inc(w12_split, 1)
                pool.tensor_copy(w2_hi[:, :, :], w2_raw[:, :, :]).then_inc(w12_split, 1)
                pool.wait_ge(w12_split, b * 4 + 2)
                pool.tensor_tensor(w1_lo[:, :, :], w1_raw[:, :, :], w1_hi[:, :, :].bitcast(F32), ALU.subtract).then_inc(w12_split, 1)
                pool.tensor_tensor(w2_lo[:, :, :], w2_raw[:, :, :], w2_hi[:, :, :].bitcast(F32), ALU.subtract).then_inc(w12_split, 1)
                pool.wait_ge(xt_mm, b * XT_N + XT_N)
                pool.wait_ge(idx_in, b * 16 + 32)
                pool.sem_inc(past, 1)
                gather()
                pool.wait_ge(xn_set, b * 2 * TT + 2 * TT)
                pool.tensor_tensor(h[:, :, :], h[:, :, :], b2_all[:, :].unsqueeze(1).broadcast_to([P, TT, D]),
                                   ALU.add).then_inc(hb_set, 1)


        @block.scalar
        def _(act):
            act.wait_ge(c_in, 16 * 6)
            with act.Fori(0, B, 1) as b:
                def std_of(n):
                    act.wait_ge(ln_var, b * 2 + n)
                    act.activation(std[:, :], mv[:, :, 1], ACT.Sqrt, bias=eps[:, 0:1]).then_inc(ln_std, 1)

                def xt_parts(n):
                    for u in range(KC * TB):
                        tb, kc = u // KC, u % KC
                        act.wait_ge(xt_mm, b * XT_N + n * KC * TB + u + 1)
                        act.activation(xt_hi[:, kc, tb * BANK:(tb + 1) * BANK], ps[:, 2 + u, :], ACT.Copy).then_inc(xt_h, 1)

                std_of(1)
                act.wait_ge(mid_out, b * 16 + 16)
                for t in range(TT):
                    act.wait_ge(got[t], b * 16 + 16)
                    act.activation(h[:, t, :], xn[:, t, :], ACT.Copy).then_inc(h_set, 1)
                xt_parts(0)
                for u in range(G * TB):
                    g, tb = u // TB, u % TB
                    act.wait_ge(qk_mm, b * G * TB + u + 1)
                    act.activation(qk_hi[:, g, tb * BANK:(tb + 1) * BANK], ps[:, PB[u] if u < 4 else 6 + u % 2, :], ACT.Identity,
                                   bias=qk_b[:, g:g + 1]).then_inc(qk_h, 1)

                for t in range(TT):
                    act.wait_ge(v_mm, b * TT + t + 1)
                    act.activation(v_sb[:, t, :, 0:HD], ps[:, 6 + t % 2, 0:D].rearrange("p (a c) -> p a c", c=HD),
                                   ACT.Copy).then_inc(v_out, 1)

                def copy_out(o):
                    act.wait_ge(pv_mm, b * G * STEPS + (o + 1) * TT)
                    if o >= 2:
                        act.wait_ge(ot_tr, b * G * TB + o - 1)
                    act.activation(ot_sb[:, o % 2, :], ps[:, 6 + o % 2, :], ACT.Copy).then_inc(ot_set, 1)

                for g in range(G):
                    for i in range(STEPS):
                        n = g * STEPS + i
                        for jp in range(2):
                            act.wait_ge(st_mm, b * G * 2 * STEPS + 2 * n + jp + 1)
                            if n >= 2:
                                act.wait_ge(pv_mm, b * G * STEPS + n - 1)
                            act.activation(p_sb[:, n % 2, 2 * jp:2 * jp + 2, :], ps[:, 2 + 2 * jp:4 + 2 * jp, :],
                                           ACT.Exp, scale=SCALE).then_inc(p_set, 1)
                        if n >= TT and n % TT == 1:
                            copy_out(n // TT - 1)
                copy_out(G * TB - 1)
                act.wait_ge(w12_split, b * 4 + 4)
                xt_parts(1)
                std_of(2)
                xt_parts(2)
                for u in range(M1 * TB):
                    m, tb = u % M1, u // M1
                    act.wait_ge(w1_mm, b * M1 * TB + u + 1)
                    if u >= 2:
                        act.wait_ge(hid_split, b * 2 * M1 * TB + 2 * (u - 1))
                    act.activation(hid_f[:, u % 2, :], ps[:, PB[u % 4], :], ACT.Relu, bias=b1_sb[:, m:m + 1]).then_inc(hid_set, 1)

        @block.vector
        def _(dve):
            dve.memset(eps[:, :], EPS)
            dve.wait_ge(w_in, 32)
            whole = []
            for kc in range(KC):
                for part in range(2):
                    whole.append((wqk_hi[:, kc, :, part * 64:(part + 1) * 64], wqk_lo[:, kc, :, part * 64:(part + 1) * 64],
                                  qkv_raw[:, kc, part * D:(part + 1) * D].rearrange("p (g c) -> p g c", g=G)))
            whole.append((wv_hi[:, :, :], wv_lo[:, :, :], qkv_raw[:, :, 2 * D:3 * D]))
            whole.append((wp_hi[:, :, :], wp_lo[:, :, :], proj_raw[:, :, :]))
            for hi, _lo, raw in whole:
                dve.tensor_copy(hi, raw).then_inc(w_split, 1)
            dve.wait_ge(w_split, len(whole))
            for hi, lo, raw in whole:
                dve.tensor_tensor(lo, raw, hi.bitcast(F32), ALU.subtract).then_inc(w_split, 1)
            dve.wait_ge(c_in, 16 * 6)
            with dve.Fori(0, B, 1) as b:
                chain = [0]
                CHAIN = 2 * (2 * TT - 1 + 1) + G * TB

                def then(ins):
                    chain[0] += 1
                    ins.then_inc(vec, 1)

                def settle():
                    dve.wait_ge(vec, b * CHAIN + chain[0])

                def row_stats(t, src):
                    then(dve.bn_stats(stats[:, t, :], src[:, t, :]))

                def normalise(n, src):
                    settle()
                    dve.sem_inc(past, 1)
                    for t in range(TT):
                        ins = dve.bn_aggr(mv[:, t, :], stats[:, t, :])
                        if t == TT - 1:
                            ins.then_inc(ln_var, 1)
                        else:
                            then(ins)
                    settle()
                    dve.wait_ge(ln_std, b * 2 + n)
                    then(dve.reciprocal(rstd[:, :], std[:, :]))
                    settle()
                    for t in range(TT):
                        if n == 1:
                            dve.wait_ge(h_set, b * TT + t + 1)
                        dve.tensor_scalar(xn[:, t, :], src[:, t, :], mv[:, t, 0:1], rstd[:, t:t + 1],
                                          ALU.subtract, ALU.mult).then_inc(xn_set, 1)

                def xt_rest(n):
                    for u in range(KC * TB):
                        tb, kc = u // KC, u % KC
                        cols = slice(tb * BANK, (tb + 1) * BANK)
                        dve.wait_ge(xt_h, b * XT_N + n * KC * TB + u + 1)
                        dve.tensor_tensor(xt_lo[:, kc, cols], ps[:, 2 + u, :], xt_hi[:, kc, cols].bitcast(F32),
                                          ALU.subtract).then_inc(xt_l, 1)

                for t in range(TT):
                    dve.wait_ge(got[t], b * 16 + 16)
                    row_stats(t, xn)
                normalise(1, xn)
                xt_rest(0)

                def qk_rest(u):
                    g, tb = u // TB, u % TB
                    cols = slice(tb * BANK, (tb + 1) * BANK)
                    dve.wait_ge(qk_h, b * G * TB + u + 1)
                    dve.scalar_tensor_tensor(out=qk_lo[:, g, cols], in0=ps[:, PB[u] if u < 4 else 6 + u % 2, :],
                                             scalar=qk_b[:, g:g + 1], in1=qk_hi[:, g, cols].bitcast(F32), op0=ALU.add,
                                             op1=ALU.subtract).then_inc(qk_l, 1)

                for u in range(FIRST):
                    qk_rest(u)

                def max_unit(u):
                    g, n = u // UNITS, u % UNITS
                    dve.wait_ge(s_mm, b * G * UNITS + u + 1)
                    dve.tensor_reduce(mx[:, g % 2, n:n + 1], ps[:, u % (RING if u < AHEAD else 2), :], AX.X,
                                      ALU.max).then_inc(s_max, 1)

                def max_pair(u):
                    dve.wait_ge(s_mm, b * G * UNITS + u + 2)
                    dve.tensor_reduce(mq[:, u // 2:u // 2 + 1], ps[:, u % RING:u % RING + 2, :], AX.XY, ALU.max).then_inc(s_max, 2)

                def group_max(g):
                    dve.wait_ge(s_max, b * G * UNITS + (g + 1) * UNITS)
                    pair = mx[:, g % 2, :].rearrange("p (n two) -> p n two", two=2)
                    dve.tensor_tensor(mq[:, :], pair[:, :, 0], pair[:, :, 1], ALU.max).then_inc(m_set, 1)

                def neg_max(g):
                    if g:
                        dve.wait_ge(nm_in, b * NMC[-1] + NMC[g - 1])
                    dve.wait_ge(m_tr, b * G + g + 1)
                    dve.tensor_scalar(nm_hi[:, :], ps[0:GH * TT, 0 if g else 7, 0:P], -1.0, None, ALU.mult).then_inc(nm_set, 1)
                    dve.wait_ge(nm_set, b * 2 * G + 2 * g + 1)
                    dve.scalar_tensor_tensor(out=nm_lo[:, :], in0=ps[0:GH * TT, 0 if g else 7, 0:P], scalar=-1.0,
                                             in1=nm_hi[:, :].bitcast(F32), op0=ALU.mult, op1=ALU.subtract).then_inc(nm_set, 1)

                def norm_out(o):
                    g, qb = o // TB, o % TB
                    dve.wait_ge(ot_tr, b * G * TB + o + 1)
                    if o:
                        dve.wait_ge(o_norm, b * G * TB + o)
                    view = ps[:, 6 + o % 2, :].rearrange("p (t j c) -> p t j c", t=4, j=GH)
                    then(dve.reciprocal(rs[:, :, :], view[:, :, :, HD]))
                    settle()
                    dve.tensor_tensor(xn[:, 4 * qb:4 * qb + 4, g * GH * HD:(g + 1) * GH * HD].rearrange(
                                          "p t (j c) -> p t j c", j=GH),
                                      view[:, :, :, 0:HD], rs[:, :, :].unsqueeze(3).broadcast_to([P, 4, GH, HD]),
                                      ALU.mult).then_inc(o_norm, 1)

                for u in range(AHEAD):
                    if u >= UNITS:
                        max_unit(u)
                    elif u % 2:
                        max_pair(u - 1)
                    k = (u - LATE) // US
                    if u % US == (US - 1 + LATE) % US and 0 <= k < G * TB - FIRST:
                        qk_rest(FIRST + k)
                    if u == UNITS + 3:
                        neg_max(0)
                for g in range(G):
                    for i in range(STEPS):
                        n = g * STEPS + i
                        for u in range(units_before(n), units_before(n + 1)):
                            max_unit(u)
                            if u % UNITS == UNITS - 1:
                                group_max(u // UNITS)
                        if n in MAXED:
                            neg_max(MAXED.index(n))
                        if n >= TT and n % TT == 3:
                            norm_out(n // TT - 1)
                norm_out(G * TB - 1)
                xt_rest(1)
                dve.wait_ge(hb_set, b * 2 + 1)
                for t in range(TT + 1):
                    if t < TT:
                        dve.wait_ge(pr_mm, b * TT + t + 1)
                        dve.tensor_tensor(h[:, t, :], ps[:, PB[t % 4], 0:D], h[:, t, :], ALU.add).then_inc(h1_set, 1)
                    if t:
                        dve.wait_ge(h1_set, b * TT + t)
                        row_stats(t - 1, h)
                normalise(2, h)
                xt_rest(2)
                for u in range(M1 * TB):
                    m, tb = u % M1, u // M1
                    cols = slice(tb * BANK, (tb + 1) * BANK)
                    dve.wait_ge(hid_set, b * M1 * TB + u + 1)
                    dve.tensor_copy(hid_hi[:, m, cols], hid_f[:, u % 2, :]).then_inc(hid_split, 1)
                    dve.wait_ge(hid_split, b * 2 * M1 * TB + 2 * u + 1)
                    dve.tensor_tensor(hid_lo[:, m, cols], hid_f[:, u % 2, :], hid_hi[:, m, cols].bitcast(F32),
                                      ALU.subtract).then_inc(hid_split, 1)
                dve.wait_ge(hb_set, b * 2 + 2)
                for t in range(TT):
                    dve.wait_ge(w2_mm, b * TT + t + 1)
                    dve.tensor_tensor(h[:, t, :], ps[:, 2 + t % 4, 0:D], h[:, t, :], ALU.add).then_inc(h2_set, 1)
                assert chain[0] == CHAIN, chain

        @block.tensor
        def _(pe):
            pe.wait_ge(id_set, 1)
            pe.wait_ge(w_split, 2 * 6)
            with pe.Fori(0, B, 1) as b:
                def transposes(n, ready):
                    for tb in range(TB):
                        for kc in range(KC):
                            for i in range(4):
                                t = 4 * tb + i
                                if kc == 0 or n == 1:
                                    ready(t)
                                ins = pe.transpose(ps[:, 2 + KC * tb + kc, i * P:(i + 1) * P], xn[:, t, kc * P:(kc + 1) * P],
                                                   ident[:, :])
                            ins.then_inc(xt_mm, 1)

                def product(out, pairs):
                    for i, (w, a) in enumerate(pairs):
                        ins = pe.matmul(out, w, a, start=(i == 0), stop=(i == len(pairs) - 1))
                    return ins

                def three(hi_a, lo_a, hi_b, lo_b):
                    return [(hi_a, hi_b), (hi_a, lo_b), (lo_a, hi_b)]

                transposes(0, lambda t: pe.wait_ge(xn_set, b * 2 * TT + t + 1))
                def qk_product(u):
                    g, tb = u // TB, u % TB
                    cols = slice(tb * BANK, (tb + 1) * BANK)
                    if u < TB:
                        pe.wait_ge(xt_h, b * XT_N + KC * (tb + 1))
                        pe.wait_ge(xt_l, b * XT_N + KC * (tb + 1))
                    if u >= 4:
                        pe.wait_ge(qk_l, b * G * TB + u - 1)
                    product(ps[:, PB[u] if u < 4 else 6 + u % 2, :],
                            [x_ for kc in range(KC) for x_ in three(wqk_hi[:, kc, g, :], wqk_lo[:, kc, g, :],
                                                                    xt_hi[:, kc, cols], xt_lo[:, kc, cols])]).then_inc(qk_mm, 1)

                def v_product(t):
                    rows = slice(t * P, (t + 1) * P)
                    if t < 2:
                        pe.wait_ge(qk_l, b * G * TB + G * TB - 1 + t)
                    else:
                        pe.wait_ge(v_out, b * TT + t - 1)
                    product(ps[:, 6 + t % 2, 0:D],
                            [x_ for kc in range(KC) for x_ in three(xt_hi[:, kc, rows], xt_lo[:, kc, rows],
                                                                    wv_hi[:, kc, :], wv_lo[:, kc, :])]).then_inc(v_mm, 1)

                def side(k):
                    if k < G * TB - FIRST:
                        qk_product(FIRST + k)
                    else:
                        v_product(k - (G * TB - FIRST))

                for u in range(FIRST):
                    qk_product(u)

                def score_unit(u):
                    hd, t, kh = u // (2 * TT), u // 2 % TT, u % 2
                    slot = hd % SLOTS
                    if u % (2 * TT) == 0:
                        uses = 2 if slot < HEADS - SLOTS else 1
                        pe.wait_ge(slot_in[slot], b * uses * HIW + (hd // SLOTS + 1) * HIW)
                        pe.wait_ge(rows_set, b * 6 + (2 if hd < GH else 4 if hd < SLOTS else 5 if hd < SLOTS + GH else 6))
                    if u == 0:
                        pe.wait_ge(qk_l, b * G * TB + FIRST)
                    ring = RING if u < AHEAD else 2
                    if u >= ring:
                        pe.wait_ge(s_max, b * G * UNITS + u - ring + 1)
                    pe.matmul(ps[:, u % ring, :], q_stack[0:KR, slot, t * P:(t + 1) * P],
                              k_stack[0:KR, slot, kh * BANK:(kh + 1) * BANK], start=True, stop=True).then_inc(s_mm, 1)

                def turn_max(g):
                    if g:
                        pe.wait_ge(m_set, b * (G - 1) + g)
                        pe.wait_ge(s_max, b * G * UNITS + (units_before(MAXED[g] + 1) - 1) // 2 * 2 + 1)
                    else:
                        pe.wait_ge(s_max, b * G * UNITS + UNITS)
                        pe.wait_ge(v_out, b * TT + TT)
                    pe.transpose(ps[0:GH * TT, 0 if g else 7, 0:P], mq[:, :], ident[:, :]).then_inc(m_tr, 1)

                def scores_t(g, i, jp):
                    qb, kt = i // TT, i % TT
                    n = g * STEPS + i
                    if i == 0 and jp == 0:
                        pe.wait_ge(nm_in, b * NMC[-1] + NMC[g])
                    if n == 0 and jp == 0:
                        pe.wait_ge(v_set, b * 2 + 2)
                        pe.wait_ge(s_max, b * G * UNITS + AHEAD)
                    if n >= 1:
                        pe.wait_ge(p_set, b * G * 2 * STEPS + 2 * n + jp - 1)
                    for j in (2 * jp, 2 * jp + 1):
                        slot = (g * GH + j) % SLOTS
                        ins = pe.matmul(ps[:, 2 + j, :], k_stack[0:KR, slot, kt * P:(kt + 1) * P],
                                        q_stack[0:KR, slot, qb * BANK:(qb + 1) * BANK], start=True, stop=True)
                    ins.then_inc(st_mm, 1)

                def values(g, i, half):
                    qb, kt = i // TT, i % TT
                    n, o = g * STEPS + i, g * TB + qb
                    cols = slice(half * BANK // 2, (half + 1) * BANK // 2)
                    if half == 0:
                        if kt == 0 and o >= 2:
                            pe.wait_ge(o_norm, b * G * TB + o - 1)
                        pe.wait_ge(p_set, b * G * 2 * STEPS + 2 * n + 2)
                    for j in range(GH):
                        ins = pe.matmul(ps[32 * j:32 * j + 2 * HD, 6 + o % 2, cols], v_sb[:, kt, g * GH + j, :],
                                        p_sb[:, n % 2, j, cols], start=(kt == 0 and half == 0), stop=(kt == TT - 1 and half == 1))
                    if half:
                        ins.then_inc(pv_mm, 1)

                def turn_out(o):
                    pe.wait_ge(ot_set, b * G * TB + o + 1)
                    for t in range(4):
                        ins = pe.transpose(ps[:, 6 + o % 2, t * P:(t + 1) * P], ot_sb[:, o % 2, t * P:(t + 1) * P], ident[:, :])
                    ins.then_inc(ot_tr, 1)

                for u in range(AHEAD):
                    score_unit(u)
                    if u % US == US - 1 and u // US < SIDES:
                        side(u // US)
                    if u == UNITS + 3:
                        turn_max(0)
                for g in range(G):
                    for i in range(STEPS):
                        n = g * STEPS + i
                        units = list(range(units_before(n), units_before(n + 1)))
                        for jp in range(2):
                            if units:
                                if n - 1 in MAXED and jp == 0:
                                    pe.wait_ge(nm_set, b * 2 * G + 2 * MAXED.index(n - 1) + 2)
                                score_unit(units[jp])
                            scores_t(g, i, jp)
                        for u in units[2:3]:
                            score_unit(u)
                        if n:
                            values((n - 1) // STEPS, (n - 1) % STEPS, 0)
                        for u in units[3:]:
                            score_unit(u)
                        if n:
                            values((n - 1) // STEPS, (n - 1) % STEPS, 1)
                        if n in MAXED:
                            turn_max(MAXED.index(n))
                        if n >= TT and n % TT == 3:
                            turn_out(n // TT - 1)
                values(G - 1, STEPS - 1, 0)
                values(G - 1, STEPS - 1, 1)
                turn_out(G * TB - 1)

                transposes(1, lambda t: pe.wait_ge(o_norm, b * G * TB + (G - 1) * TB + t // 4 + 1))
                pe.wait_ge(xt_h, b * XT_N + 2 * KC * TB)
                pe.wait_ge(xt_l, b * XT_N + 2 * KC * TB)
                for t in range(TT):
                    rows = slice(t * P, (t + 1) * P)
                    if t >= 4:
                        pe.wait_ge(h1_set, b * TT + t - 3)
                    product(ps[:, PB[t % 4], 0:D],
                            [x_ for kc in range(KC) for x_ in three(xt_hi[:, kc, rows], xt_lo[:, kc, rows],
                                                                    wp_hi[:, kc, :], wp_lo[:, kc, :])]).then_inc(pr_mm, 1)
                transposes(2, lambda t: pe.wait_ge(xn_set, b * 2 * TT + TT + t + 1))
                pe.wait_ge(w12_split, b * 4 + 4)
                for u in range(M1 * TB):
                    m, tb = u % M1, u // M1
                    cols = slice(tb * BANK, (tb + 1) * BANK)
                    if m == 0:
                        pe.wait_ge(xt_h, b * XT_N + 2 * KC * TB + KC * (tb + 1))
                        pe.wait_ge(xt_l, b * XT_N + 2 * KC * TB + KC * (tb + 1))
                    if u >= 4:
                        pe.wait_ge(hid_set, b * M1 * TB + u - 3)
                    mc = slice(m * P, (m + 1) * P)
                    product(ps[:, PB[u % 4], :],
                            [x_ for kc in range(KC) for x_ in three(w1_hi[:, kc, mc], w1_lo[:, kc, mc],
                                                                    xt_hi[:, kc, cols], xt_lo[:, kc, cols])]).then_inc(w1_mm, 1)
                for t in range(TT):
                    rows = slice(t * P, (t + 1) * P)
                    if t % 4 == 0:
                        pe.wait_ge(hid_split, b * 2 * M1 * TB + 2 * M1 * (t // 4 + 1))
                    if t >= 4:
                        pe.wait_ge(h2_set, b * TT + t - 3)
                    product(ps[:, 2 + t % 4, 0:D],
                            [x_ for m in range(M1) for x_ in three(hid_hi[:, m, rows], hid_lo[:, m, rows],
                                                                   w2_hi[:, m, :], w2_lo[:, m, :])]).then_inc(w2_mm, 1)


def second_layer(nc, h_mid, wq, bq, wv, bv, anomaly, enc_w, enc_b, s2c_w, s2c_b, r_w1, r_b1, r_w2, r_b2, e_w1, e_b1, e_w2,
          e_b2, c2s_w, c2s_b, dec_w, dec_b, ln_g, ln_b, out, early, raw_in):
    B, N, D = h_mid.shape
    KC = D // P
    TT = N // P
    TB = N // BANK
    HID = enc_w.shape[1]
    MH = HID // P
    C = s2c_w.shape[1]
    E = r_w2.shape[1]
    EH = e_w1.shape[2] // P
    PAIRS = E // 2
    SCALE = float(D) ** -0.5
    EPS = 1e-5
    ctx = ExitStack()
    with ctx:
        base = (nc.sbuf_base + 31) // 32 * 32
        top = [base]

        def at(name, shape, dt, offset=None):
            size = 4
            for n in shape[1:]:
                size *= n
            if offset is None:
                offset = top[0]
                top[0] += (size + 31) // 32 * 32
            return nc.alloc_sbuf_tensor_at(name, shape, dt, offset=offset)

        h = at("u_h", [P, TT, D], F32)
        xn = at("u_xn", [P, TT, D], F32)
        xt_hi = at("u_xt_hi", [P, KC, N], F32R)
        xt_lo_at = top[0]
        xt_lo = at("u_xt_lo", [P, KC, N], F32R)
        h_next = at("h_next", [P, TT, D], F32, xt_lo_at)
        raw_at = top[0]
        qt_hi = at("qt_hi", [P, KC, N], F32R)
        qt_lo = at("qt_lo", [P, KC, N], F32R)
        tq_hi = at("tq_hi", [P, KC, N], F32R)
        tq_lo = at("tq_lo", [P, KC, N], F32R)
        v_f = at("v_f", [P, TT, D], F32)
        v_hi = at("v_hi", [P, TT, D], F32R)
        v_lo = at("v_lo", [P, TT, D], F32R)
        pr = at("pr", [P, 2, N], F32)
        pt_hi = at("pt_hi", [P, 2, TT, P], F32R)
        pt_lo = at("pt_lo", [P, 2, TT, P], F32R)
        end = top[0]
        top[0] = raw_at
        sp_hi = at("sp_hi", [P, MH, N], F32R)
        sp_lo = at("sp_lo", [P, MH, N], F32R)
        rt_hi, rt_lo = (nc.alloc_sbuf_tensor_at(n, [P, MH, N], F32R, offset=raw_at + i * 4 * MH * N)
                        for i, n in enumerate(("rt_hi", "rt_lo")))
        cs = at("cs", [P, N], F32R)
        rs = at("u_rs", [P, N], F32R)
        eh = at("eh", [P, 8, BANK], F32)
        cb = at("cb", [P, 2, BANK], F32)
        y = at("y", [P, BANK], F32)
        ysum = at("ysum", [P, TB, BANK], F32)
        ys_hi = at("ys_hi", [P, N], F32R)
        ys_lo = at("ys_lo", [P, N], F32R)
        dd = xn
        assert top[0] <= end, (top[0], end)
        wq_raw, wv_raw, an_raw = early
        top[0] = end
        f_sb = at("f_sb", [P, 2, BANK], F32)
        ch = at("ch", [P, BANK], F32R)
        wqt_hi = at("wqt_hi", [P, KC, D], F32R)
        wqt_lo = at("wqt_lo", [P, KC, D], F32R)
        wvt_hi = at("wvt_hi", [P, KC, D], F32R)
        wvt_lo = at("wvt_lo", [P, KC, D], F32R)
        an_hi = at("an_hi", [P, KC, D], F32R)
        an_lo = at("an_lo", [P, KC, D], F32R)
        enc_hi = at("enc_hi", [P, KC, HID], F32R)
        enc_lo = at("enc_lo", [P, KC, HID], F32R)
        s2c_hi = at("s2c_hi", [P, MH, 2, C], F32R)
        s2c_lo = at("s2c_lo", [P, MH, 2, C], F32R)
        rw1_hi = at("rw1_hi", [P, 2, C], F32R)
        rw1_lo = at("rw1_lo", [P, 2, C], F32R)
        rw2_hi = at("rw2_hi", [P, E], F32R)
        rw2_lo = at("rw2_lo", [P, E], F32R)
        ew1_hi = at("ew1_hi", [P, E, EH * P], F32R)
        ew1_lo = at("ew1_lo", [P, E, EH * P], F32R)
        ew2_sb = at("ew2_sb", [P, E, EH, C], F32)
        c2s_hi = at("c2s_hi", [P, HID], F32R)
        c2s_lo = at("c2s_lo", [P, HID], F32R)
        dec_hi = at("dec_hi", [P, MH, D], F32R)
        dec_lo = at("dec_lo", [P, MH, D], F32R)
        ident = at("u_ident", [P, P], F32)
        bv_all = at("u_bv", [P, D], F32)
        decb_all = at("decb_all", [P, D], F32)
        g_all = at("g_all", [P, D], F32)
        lnb_all = at("lnb_all", [P, D], F32)
        rb2_all = at("rb2_all", [P, E], F32)
        bq_sb = at("bq_sb", [P, KC], F32)
        encb = at("encb", [P, MH], F32)
        s2cb = at("s2cb", [P, 1], F32)
        rb1 = at("rb1", [P, 1], F32)
        eb1 = at("eb1", [P, E, EH], F32)
        eb2 = at("eb2", [P, PAIRS], F32)
        c2sb = at("c2sb", [P, MH], F32)
        desc = at("desc", [P, E], F32)
        stats = at("u_stats", [P, TT, 6], F32)
        mv = at("u_mv", [P, TT, 2], F32)
        rstd = at("u_rstd", [P, TT], F32)
        std = at("u_std", [P, TT], F32)
        eps = at("u_eps", [P, 1], F32)
        nrc = at("nrc", [P, TT], F32)
        nrm = at("nrm", [P, TT], F32)
        nrd = at("nrd", [P, TT], F32)
        rn = at("rn", [P, TT], F32)
        smax = at("smax", [P, TT], F32)
        nb = at("nb", [P, TT], F32)
        sums = at("sums", [P, TT], F32)
        rsum = at("rsum", [P, TT], F32)
        cf = at("cf", [P, TT], F32)
        small = [at(f"small{i}", [P, TT, E], F32) for i in range(6)]
        gate_at = top[0]
        gate_w = at("gate_w", [P, TT, E, C], F32)
        gate_end = top[0]
        top[0] = gate_at
        enc_raw = at("enc_raw", [P, KC, HID], F32)
        ew1_raw = at("ew1_raw", [P, E, EH * P], F32)
        dec_raw = at("dec_raw", [P, MH, D], F32)
        assert top[0] <= gate_end
        top[0] = gate_end
        s2c_raw = at("s2c_raw", [P, MH, C], F32)
        rw1_raw = at("rw1_raw", [P, C], F32)
        rw2_raw = at("rw2_raw", [P, E], F32)
        c2s_raw = at("c2s_raw", [P, HID], F32)
        tiny = [at(f"tiny{i}", [P, TT], F32) for i in range(5)]
        assert top[0] <= EARLY_AT, top[0]
        ps = ctx.enter_context(nc.psum_tensor("u_ps", [P, 8, BANK], F32))

        def sem(name):
            return ctx.enter_context(nc.semaphore("u_" + name))

        raw2_in = sem("raw2_in")
        bq_in = sem("bq_in")
        bv_in = sem("bv_in")
        f_hi = sem("f_hi")
        f_lo = sem("f_lo")
        c_in = sem("c_in")
        id0 = sem("id0")
        id_set = sem("id_set")
        wt_mm = sem("wt_mm")
        w_hi = sem("w_hi")
        an_set = sem("an_set")
        w_set = sem("w_set")
        h_in = sem("h_in")
        h_res_in = sem("h_res_in")
        past = sem("past")
        vec = sem("vec")
        ln_var = sem("ln_var")
        ln_std = sem("ln_std")
        n_set = sem("n_set")
        xn_set = sem("xn_set")
        xt_mm = sem("xt_mm")
        xt_h = sem("xt_h")
        xt_l = sem("xt_l")
        q_mm = sem("q_mm")
        q_h = sem("q_h")
        q_l = sem("q_l")
        v_mm = sem("v_mm")
        v_set = sem("v_set")
        v_parts = sem("v_parts")
        s_mm = sem("s_mm")
        nb_set = sem("nb_set")
        p_set = sem("p_set")
        pt_mm = sem("pt_mm")
        pt_h = sem("pt_h")
        pt_l = sem("pt_l")
        pv_mm = sem("pv_mm")
        h_set = sem("h_set")
        f_mm = sem("f_mm")
        f_set = sem("f_set")
        f_split = sem("f_split")
        lg_mm = sem("lg_mm")
        lg_set = sem("lg_set")
        eg_set = sem("eg_set")
        comb_set = sem("comb_set")
        gate_set = sem("gate_set")
        cb_mm = sem("cb_mm")
        cb_set = sem("cb_set")
        e1_mm = sem("e1_mm")
        eh_set = sem("eh_set")
        e2_mm = sem("e2_mm")
        y_set = sem("y_set")
        ys_set = sem("ys_set")
        de_mm = sem("de_mm")
        de_set = sem("de_set")
        dd_set = sem("dd_set")
        hb_set = sem("hb_set")
        out_set = sem("out_set")
        stored = sem("stored")
        RAWS = 3
        RAWS2 = 11
        CONSTS = 14
        FU = 2 * TB * MH + 2 * TB
        PB = (0, 1, 6, 7)

        def split_list():
            jobs = [(enc_hi[:, :, :], enc_lo[:, :, :], enc_raw[:, :, :])]
            for i in range(2):
                jobs.append((s2c_hi[:, :, i, :], s2c_lo[:, :, i, :], s2c_raw[:, :, :]))
                jobs.append((rw1_hi[:, i, :], rw1_lo[:, i, :], rw1_raw[:, :]))
            jobs.append((rw2_hi[:, :], rw2_lo[:, :], rw2_raw[:, :]))
            jobs.append((ew1_hi[:, :, :], ew1_lo[:, :, :], ew1_raw[:, :, :]))
            jobs.append((c2s_hi[:, :], c2s_lo[:, :], c2s_raw[:, :]))
            jobs.append((dec_hi[:, :, :], dec_lo[:, :, :], dec_raw[:, :, :]))
            return jobs

        SPLITS = 2
        SPLITS2 = len(split_list())

        block = ctx.enter_context(nc.Block())

        @block.sync
        def _(sp):
            def load(dst, src, s=c_in):
                sp.dma_start(dst, src).then_inc(s, 16)

            def load_rows(b):
                sp.dma_start(h_next[:, :, :], h_mid[bass.ds(b, 1)].rearrange("o (p t) d -> p (o t) d", p=P)).then_inc(h_in, 16)

            def load_residual(b):
                sp.wait_ge(stored, b * 32 + 16)
                sp.dma_start(h[:, :, :], h_mid[bass.ds(b, 1)].rearrange("o (p t) d -> p (o t) d", p=P)).then_inc(h_res_in, 16)

            def store_rows(b):
                rows = out[bass.ds(b, 1)].rearrange("o (p t) d -> p (o t) d", p=P)
                for half in range(2):
                    tiles = slice(half * TT // 2, (half + 1) * TT // 2)
                    sp.wait_ge(out_set, b * TT + (half + 1) * TT // 2)
                    sp.dma_start(rows[:, tiles, :], h[:, tiles, :]).then_inc(stored, 16)

            load_rows(0)
            load(bv_all[:, :], bv.partition_broadcast(P), bv_in)
            with nc.allow_non_contiguous_dma("biases by partition"):
                load(bq_sb[:, :], bq.rearrange("(k p) -> p k", p=P), bq_in)
            load(s2c_raw[:, :, :], s2c_w.rearrange("(k p) n -> p k n", p=P), raw2_in)
            for i in range(2):
                half = slice(i * C, (i + 1) * C)
                load(rw1_raw[half, :], r_w1, raw2_in)
                load(rw2_raw[half, :], r_w2, raw2_in)
                load(c2s_raw[half, :], c2s_w, raw2_in)
                load(ew1_raw[half, :, :], e_w1.rearrange("e d h -> d e h"), raw2_in)
            load(enc_raw[:, :, :], enc_w.rearrange("(k p) n -> p k n", p=P), raw2_in)
            load(dec_raw[:, :, :], dec_w.rearrange("(k p) n -> p k n", p=P), raw2_in)
            load(ew2_sb[:, :, :, :], e_w2.rearrange("e (k p) d -> p e k d", p=P))
            with nc.allow_non_contiguous_dma("biases by partition"):
                load(encb[:, :], enc_b.rearrange("(k p) -> p k", p=P))
                load(c2sb[:, :], c2s_b.rearrange("(k p) -> p k", p=P))
                load(eb1[:, :, :], e_b1.rearrange("e (k p) -> p e k", p=P))
                for i in range(2):
                    half = slice(i * C, (i + 1) * C)
                    load(s2cb[half, :], s2c_b.rearrange("(c o) -> c o", o=1))
                    load(rb1[half, :], r_b1.rearrange("(c o) -> c o", o=1))
                    load(eb2[half, :], e_b2.rearrange("(q two) d -> two d q", two=2)[i])
            for dst, src in ((decb_all, dec_b), (g_all, ln_g), (lnb_all, ln_b), (rb2_all, r_b2)):
                load(dst[:, :], src.partition_broadcast(P))
            sp.sem_inc(stored, 16)
            load_residual(0)
            with sp.Fori(0, B - 1, 1) as b:
                sp.wait_ge(f_mm, b * FU + TB * MH)
                load_rows(b + 1)
                store_rows(b)
                load_residual(b + 1)
            store_rows(B - 1)
            sp.wait_ge(stored, 32 * B + 16)

        @block.gpsimd
        def _(pool):
            pool.memset(ident[:, :], 0.0).then_inc(id0, 1)
            pool.wait_ge(id0, 1)
            pool.affine_select(out=ident[:, :], in_=ident[:, :], compare_op=ALU.not_equal, fill=1.0, base=0,
                               pattern=[[-1, P]], channel_multiplier=1).then_inc(id_set, 1)
            pool.iota(desc[:, :], pattern=[[-1, E]], base=E, channel_multiplier=0,
                      allow_small_or_imprecise_dtypes=True).then_inc(id_set, 1)
            pool.wait_ge(raw_in, 16 * RAWS)
            pool.tensor_copy(an_hi[:, :, :], an_raw[:, :, :]).then_inc(an_set, 1)
            pool.wait_ge(an_set, 1)
            pool.tensor_tensor(an_lo[:, :, :], an_raw[:, :, :], an_hi[:, :, :].bitcast(F32), ALU.subtract).then_inc(an_set, 1)
            pool.wait_ge(raw2_in, 16 * RAWS2)
            for hi, _lo, raw in split_list():
                pool.tensor_copy(hi, raw).then_inc(f_hi, 1)
            pool.wait_ge(f_hi, SPLITS2)
            for hi, lo, raw in split_list():
                pool.tensor_tensor(lo, raw, hi.bitcast(F32), ALU.subtract).then_inc(f_lo, 1)
            pool.wait_ge(f_lo, SPLITS2)
            pool.wait_ge(c_in, 16 * CONSTS)
            with pool.Fori(0, B, 1) as b:
                pool.wait_ge(comb_set, b + 1)
                pool.sem_inc(past, 1)
                for v in range(TB * PAIRS):
                    tiles = slice(v // PAIRS * 4, v // PAIRS * 4 + 4)
                    pair = slice(2 * (v % PAIRS), 2 * (v % PAIRS) + 2)
                    pool.tensor_copy(gate_w[:, tiles, pair, :], small[5][:, tiles, pair].unsqueeze(3).broadcast_to(
                        [P, 4, 2, C])).then_inc(gate_set, 1)
                pool.wait_ge(xn_set, b * 2 * TT + 2 * TT)
                pool.tensor_tensor(h[:, :, :], h[:, :, :], lnb_all[:, :].unsqueeze(1).broadcast_to([P, TT, D]),
                                   ALU.add).then_inc(hb_set, 1)

        @block.scalar
        def _(act):
            for i, hi in enumerate((wqt_hi, wvt_hi)):
                act.wait_ge(wt_mm, i + 1)
                act.activation(hi[:, :, :].rearrange("p k n -> p (k n)"), ps[:, i, :], ACT.Copy).then_inc(w_hi, 1)
            act.wait_ge(bq_in, 16)
            with act.Fori(0, B, 1) as b:
                def std_of(n, tiles=slice(0, TT)):
                    act.wait_ge(ln_var, b * 4 + n)
                    act.activation(std[:, tiles], mv[:, tiles, 1], ACT.Sqrt, bias=eps[:, 0:1]).then_inc(ln_std, 1)

                def xt_parts(n):
                    for u in range(KC * TB):
                        tb, kc = u // KC, u % KC
                        act.wait_ge(xt_mm, b * 2 * KC * TB + n * KC * TB + u + 1)
                        act.activation(xt_hi[:, kc, tb * BANK:(tb + 1) * BANK], ps[:, 2 + u, :], ACT.Copy).then_inc(xt_h, 1)

                std_of(1)
                act.activation(nrc[:, :], mv[:, :, 1], ACT.Sqrt, scale=float(D)).then_inc(n_set, 1)
                xt_parts(0)
                for u in range(2 * KC * TB):
                    kc, tb = u // TB % KC, u % TB
                    cols = slice(tb * BANK, (tb + 1) * BANK)
                    act.wait_ge(q_mm, b * 2 * KC * TB + u + 1)
                    if u < KC * TB:
                        act.activation(qt_hi[:, kc, cols], ps[:, PB[u % 4], :], ACT.Identity, bias=bq_sb[:, kc:kc + 1]).then_inc(q_h, 1)
                    else:
                        act.activation(tq_hi[:, kc, cols], ps[:, PB[u % 4], :], ACT.Copy).then_inc(q_h, 1)

                def parts_of_p(t):
                    act.wait_ge(pt_mm, b * TT + t + 1)
                    if t >= 2:
                        act.wait_ge(pv_mm, b * TT + t - 1)
                    act.activation(pt_hi[:, t % 2, :, :].rearrange("p a c -> p (a c)"),
                                   ps[:, 2 + 2 * (t % 2):4 + 2 * (t % 2), :].rearrange("p a c -> p (a c)"), ACT.Copy).then_inc(pt_h, 1)

                for t in range(TT):
                    act.wait_ge(nb_set, b * TT + t + 1)
                    if t >= 2:
                        act.wait_ge(pt_mm, b * TT + t - 1)
                    act.activation(pr[:, t % 2, :], ps[:, 0:2, :].rearrange("p a c -> p (a c)"), ACT.Exp, bias=nb[:, t:t + 1],
                                   scale=SCALE, accum_out=sums[:, t:t + 1]).then_inc(p_set, 1)
                    if t == 0:
                        act.wait_ge(v_set, b * TT + TT)
                        act.activation(v_hi[:, :, :], v_f[:, :, :], ACT.Copy).then_inc(v_parts, 1)
                    if t:
                        parts_of_p(t - 1)
                parts_of_p(TT - 1)
                std_of(2)
                xt_parts(1)
                act.wait_ge(c_in, 16 * CONSTS)

                def after(u, bank, func, bias):
                    act.wait_ge(f_mm, b * FU + u + 1)
                    if u >= 2:
                        act.wait_ge(f_split, b * FU + u - 1)
                    act.activation(f_sb[:, u % 2, :], ps[:, bank, :], func, bias=bias).then_inc(f_set, 1)

                for u in range(TB * MH):
                    after(u, PB[u % 4], ACT.Sigmoid, encb[:, u % MH:u % MH + 1])
                for tb in range(TB):
                    after(TB * MH + tb, 2 + tb, ACT.Identity, s2cb[:, 0:1])
                for tb in range(TB):
                    after(TB * MH + TB + tb, 4 + tb, ACT.Relu, rb1[:, 0:1])
                act.wait_ge(lg_set, b + 1)
                act.activation(small[1][:, :, :], small[0][:, :, :], ACT.Exp).then_inc(eg_set, 1)

                def hidden(n):
                    act.wait_ge(e1_mm, b * TB * E * EH + n + 1)
                    if n >= 8:
                        act.wait_ge(e2_mm, b * TB * PAIRS + (n - 8) // 4 + 1)
                    act.activation(eh[:, n % 8, :], ps[:, n % 2, :], ACT.Relu, bias=eb1[:, n // EH % E, n % EH:n % EH + 1]).then_inc(eh_set, 1)

                def gate(v):
                    act.wait_ge(cb_mm, b * TB * PAIRS + v + 1)
                    if v >= 2:
                        act.wait_ge(y_set, b * TB * PAIRS + v - 1)
                    act.activation(cb[:, v % 2, :], ps[:, 4 + v % 2, :], ACT.Copy).then_inc(cb_set, 1)

                for v in range(TB * PAIRS + 1):
                    if v < TB * PAIRS:
                        for n in range(4 * v, 4 * v + 4):
                            hidden(n)
                    if v:
                        gate(v - 1)
                for u in range(TB * MH):
                    after(TB * MH + 2 * TB + u, PB[u % 4], ACT.Sigmoid, c2sb[:, u % MH:u % MH + 1])
                for half in range(2):
                    for t in range(half * TT // 2, (half + 1) * TT // 2):
                        act.wait_ge(de_set, b * TT + t + 1)
                        act.activation(dd[:, t, :], dd[:, t, :], ACT.Sigmoid).then_inc(dd_set, 1)
                    std_of(3 + half, slice(half * TT // 2, (half + 1) * TT // 2))

        @block.vector
        def _(dve):
            dve.memset(eps[:, :], EPS)
            for i, (hi, lo) in enumerate(((wqt_hi, wqt_lo), (wvt_hi, wvt_lo))):
                dve.wait_ge(w_hi, i + 1)
                dve.tensor_tensor(lo[:, :, :].rearrange("p k n -> p (k n)"), ps[:, i, :],
                                  hi[:, :, :].rearrange("p k n -> p (k n)").bitcast(F32), ALU.subtract).then_inc(w_set, 1)
            dve.wait_ge(w_set, SPLITS)
            dve.wait_ge(id_set, 2)
            dve.wait_ge(bv_in, 16)
            with dve.Fori(0, B, 1) as b:
                chain = [0]
                CHAIN = 3 * 2 * TT + 4 + TT * 3 + TT + 37 + TB * (PAIRS + 1) + 2

                def then(ins):
                    chain[0] += 1
                    ins.then_inc(vec, 1)

                def settle():
                    dve.wait_ge(vec, b * CHAIN + chain[0])

                def step(ins):
                    then(ins)
                    settle()

                def row_stats(t, src):
                    then(dve.bn_stats(stats[:, t, :], src[:, t, :]))

                def moments(n, first=0, last=TT):
                    settle()
                    dve.sem_inc(past, 1)
                    for t in range(first, last):
                        ins = dve.bn_aggr(mv[:, t, :], stats[:, t, :])
                        if t == last - 1:
                            ins.then_inc(ln_var, 1)
                        else:
                            then(ins)
                    settle()
                    dve.wait_ge(ln_std, b * 4 + n)
                    step(dve.reciprocal(rstd[:, first:last], std[:, first:last]))

                def xt_rest(n):
                    for u in range(KC * TB):
                        tb, kc = u // KC, u % KC
                        cols = slice(tb * BANK, (tb + 1) * BANK)
                        dve.wait_ge(xt_h, b * 2 * KC * TB + n * KC * TB + u + 1)
                        dve.tensor_tensor(xt_lo[:, kc, cols], ps[:, 2 + u, :], xt_hi[:, kc, cols].bitcast(F32),
                                          ALU.subtract).then_inc(xt_l, 1)

                dve.wait_ge(h_in, b * 16 + 16)
                for t in range(TT):
                    row_stats(t, h_next)
                moments(1)
                dve.wait_ge(n_set, b + 1)
                step(dve.tensor_tensor(nrm[:, :], nrc[:, :], rstd[:, :], ALU.mult))
                step(dve.tensor_scalar(nrd[:, :], nrm[:, :], 1e-9, None, ALU.add))
                step(dve.reciprocal(rn[:, :], nrd[:, :]))
                step(dve.tensor_tensor(rn[:, :], rn[:, :], rstd[:, :], ALU.mult))
                for t in range(TT):
                    dve.tensor_scalar(xn[:, t, :], h_next[:, t, :], mv[:, t, 0:1], rn[:, t:t + 1],
                                      ALU.subtract, ALU.mult).then_inc(xn_set, 1)
                dve.wait_ge(xn_set, b * 2 * TT + TT)
                xt_rest(0)
                for u in range(2 * KC * TB):
                    kc, tb = u // TB % KC, u % TB
                    cols = slice(tb * BANK, (tb + 1) * BANK)
                    dve.wait_ge(q_h, b * 2 * KC * TB + u + 1)
                    if u < KC * TB:
                        dve.scalar_tensor_tensor(out=qt_lo[:, kc, cols], in0=ps[:, PB[u % 4], :], scalar=bq_sb[:, kc:kc + 1],
                                                 in1=qt_hi[:, kc, cols].bitcast(F32), op0=ALU.add, op1=ALU.subtract).then_inc(q_l, 1)
                    else:
                        dve.tensor_tensor(tq_lo[:, kc, cols], ps[:, PB[u % 4], :], tq_hi[:, kc, cols].bitcast(F32),
                                          ALU.subtract).then_inc(q_l, 1)
                def v_bias():
                    for t in range(TT):
                        dve.wait_ge(v_mm, b * TT + t + 1)
                        dve.tensor_tensor(v_f[:, t, :], ps[:, 2 + t % 4, 0:D], bv_all[:, :], ALU.add).then_inc(v_set, 1)

                def v_rest():
                    dve.wait_ge(v_parts, b * 2 + 1)
                    dve.tensor_tensor(v_lo[:, :, :], v_f[:, :, :], v_hi[:, :, :].bitcast(F32), ALU.subtract).then_inc(v_parts, 1)

                def rest_of_p(t):
                    dve.wait_ge(pt_h, b * TT + t + 1)
                    dve.tensor_tensor(pt_lo[:, t % 2, :, :].rearrange("p a c -> p (a c)"),
                                      ps[:, 2 + 2 * (t % 2):4 + 2 * (t % 2), :].rearrange("p a c -> p (a c)"),
                                      pt_hi[:, t % 2, :, :].rearrange("p a c -> p (a c)").bitcast(F32), ALU.subtract).then_inc(pt_l, 1)

                def context(t):
                    step(dve.reciprocal(rsum[:, t:t + 1], sums[:, t:t + 1]))
                    step(dve.tensor_tensor(cf[:, t:t + 1], rsum[:, t:t + 1], nrm[:, t:t + 1], ALU.mult))
                    dve.wait_ge(pv_mm, b * TT + t + 1)
                    dve.scalar_tensor_tensor(out=h[:, t, :], in0=ps[:, 6 + t % 2, 0:D], scalar=cf[:, t:t + 1],
                                             in1=h[:, t, :], op0=ALU.mult, op1=ALU.add).then_inc(h_set, 1)

                dve.wait_ge(h_res_in, b * 16 + 16)
                for t in range(TT):
                    dve.wait_ge(s_mm, b * TT + t + 1)
                    step(dve.tensor_reduce(smax[:, t:t + 1], ps[:, 0:2, :], AX.XY, ALU.max))
                    dve.tensor_scalar(nb[:, t:t + 1], smax[:, t:t + 1], -SCALE, None, ALU.mult).then_inc(nb_set, 1)
                    if t == 0:
                        v_bias()
                    if t == 1:
                        v_rest()
                    if t:
                        rest_of_p(t - 1)
                    if t >= 2:
                        context(t - 2)
                    if t >= 3:
                        dve.wait_ge(h_set, b * TT + t - 2)
                        row_stats(t - 3, h)
                rest_of_p(TT - 1)
                context(TT - 2)
                for t in range(TT - 3, TT - 1):
                    dve.wait_ge(h_set, b * TT + t + 1)
                    row_stats(t, h)
                context(TT - 1)
                dve.wait_ge(h_set, b * TT + TT)
                row_stats(TT - 1, h)
                moments(2)
                for t in range(TT):
                    dve.tensor_scalar(xn[:, t, :], h[:, t, :], mv[:, t, 0:1], rstd[:, t:t + 1],
                                      ALU.subtract, ALU.mult).then_inc(xn_set, 1)
                xt_rest(1)
                dve.wait_ge(c_in, 16 * CONSTS)

                def parts(u, hi, lo):
                    dve.wait_ge(f_set, b * FU + u + 1)
                    step(dve.tensor_copy(hi, f_sb[:, u % 2, :]))
                    dve.tensor_tensor(lo, f_sb[:, u % 2, :], hi.bitcast(F32), ALU.subtract).then_inc(f_split, 1)

                def stacked(u, dst):
                    dve.wait_ge(f_set, b * FU + u + 1)
                    then(dve.tensor_copy(dst[0:C, :], f_sb[0:C, u % 2, :]))
                    step(dve.tensor_copy(ch[C:P, :], f_sb[C:P, u % 2, :]))
                    dve.tensor_tensor(dst[C:P, :], f_sb[C:P, u % 2, :], ch[C:P, :].bitcast(F32), ALU.subtract).then_inc(f_split, 1)

                for u in range(TB * MH):
                    tb, m = u // MH, u % MH
                    cols = slice(tb * BANK, (tb + 1) * BANK)
                    parts(u, sp_hi[:, m, cols], sp_lo[:, m, cols])
                for tb in range(TB):
                    dve.wait_ge(f_split, b * FU + TB * MH + tb)
                    stacked(TB * MH + tb, cs[:, tb * BANK:(tb + 1) * BANK])
                for tb in range(TB):
                    dve.wait_ge(f_split, b * FU + TB * MH + TB + tb)
                    stacked(TB * MH + TB + tb, rs[:, tb * BANK:(tb + 1) * BANK])
                lg, eg, one, two, tmp, comb = (s[:, :, :] for s in small)
                m1, r1, m2, r2, den = (s[:, :] for s in tiny)

                def wide(s):
                    return s.unsqueeze(2).broadcast_to([P, TT, E])

                order = desc[:, :].unsqueeze(1).broadcast_to([P, TT, E])
                dve.wait_ge(lg_mm, b + 1)
                step(dve.tensor_tensor(tmp, ps[:, 2, 0:TT * E].rearrange("p (t e) -> p t e", e=E),
                                       rb2_all[:, :].unsqueeze(1).broadcast_to([P, TT, E]), ALU.add))
                step(dve.tensor_reduce(m1, tmp, AX.X, ALU.max))
                dve.tensor_tensor(lg, tmp, wide(m1), ALU.subtract).then_inc(lg_set, 1)
                dve.wait_ge(eg_set, b + 1)
                step(dve.tensor_reduce(m1, eg, AX.X, ALU.max))
                step(dve.tensor_tensor(tmp, eg, wide(m1), ALU.is_equal))
                step(dve.tensor_tensor(tmp, tmp, order, ALU.mult))
                step(dve.tensor_reduce(r1, tmp, AX.X, ALU.max))
                step(dve.tensor_tensor(one, order, wide(r1), ALU.is_equal))
                step(dve.scalar_tensor_tensor(out=two, in0=one, scalar=-2.0, in1=eg, op0=ALU.mult, op1=ALU.add))
                step(dve.tensor_reduce(m2, two, AX.X, ALU.max))
                step(dve.tensor_tensor(tmp, two, wide(m2), ALU.is_equal))
                step(dve.tensor_tensor(tmp, tmp, order, ALU.mult))
                step(dve.tensor_reduce(r2, tmp, AX.X, ALU.max))
                step(dve.tensor_tensor(two, order, wide(r2), ALU.is_equal))
                step(dve.tensor_tensor(one, one, two, ALU.add))
                step(dve.tensor_tensor(one, one, eg, ALU.mult))
                step(dve.tensor_tensor(den, m1, m2, ALU.add))
                step(dve.reciprocal(r1, den))
                dve.tensor_tensor(comb, one, wide(r1), ALU.mult).then_inc(comb_set, 1)
                for v in range(TB * PAIRS):
                    tb, q = v // PAIRS, v % PAIRS
                    dve.wait_ge(e2_mm, b * TB * PAIRS + v + 1)
                    dve.wait_ge(cb_set, b * TB * PAIRS + v + 1)
                    if q:
                        settle()
                        dve.scalar_tensor_tensor(out=y[:, :], in0=ps[:, 6 + v % 2, :], scalar=eb2[:, q:q + 1], in1=cb[:, v % 2, :],
                                                 op0=ALU.add, op1=ALU.mult).then_inc(y_set, 1)
                        dve.wait_ge(y_set, b * TB * PAIRS + v + 1)
                        then(dve.tensor_tensor(ysum[:, tb, :], ysum[:, tb, :], y[:, :], ALU.add))
                    else:
                        dve.scalar_tensor_tensor(out=ysum[:, tb, :], in0=ps[:, 6 + v % 2, :], scalar=eb2[:, q:q + 1],
                                                 in1=cb[:, v % 2, :], op0=ALU.add, op1=ALU.mult).then_inc(y_set, 1)
                        dve.wait_ge(y_set, b * TB * PAIRS + v + 1)
                    if q == PAIRS - 1:
                        settle()
                        cols = slice(tb * BANK, (tb + 1) * BANK)
                        step(dve.tensor_copy(ys_hi[:, cols], ysum[:, tb, :]))
                        dve.tensor_tensor(ys_lo[:, cols], ysum[:, tb, :], ys_hi[:, cols].bitcast(F32), ALU.subtract).then_inc(ys_set, 1)
                for u in range(TB * MH):
                    tb, m = u // MH, u % MH
                    cols = slice(tb * BANK, (tb + 1) * BANK)
                    parts(TB * MH + 2 * TB + u, rt_hi[:, m, cols], rt_lo[:, m, cols])
                for half in range(2):
                    first, last = half * TT // 2, (half + 1) * TT // 2
                    for t in range(first, last + 2):
                        if t < last:
                            dve.wait_ge(de_mm, b * TT + t + 1)
                            dve.tensor_tensor(dd[:, t, :], ps[:, 2 + t % 4, 0:D], decb_all[:, :], ALU.add).then_inc(de_set, 1)
                        if t >= first + 2:
                            dve.wait_ge(dd_set, b * TT + t - 1)
                            row_stats(t - 2, dd)
                    moments(3 + half, first, last)
                    for t in range(first, last):
                        then(dve.scalar_tensor_tensor(out=dd[:, t, :], in0=dd[:, t, :], scalar=mv[:, t, 0:1], in1=g_all[:, :],
                                                      op0=ALU.subtract, op1=ALU.mult))
                    settle()
                    dve.wait_ge(hb_set, b + 1)
                    for t in range(first, last):
                        dve.scalar_tensor_tensor(out=h[:, t, :], in0=dd[:, t, :], scalar=rstd[:, t:t + 1], in1=h[:, t, :],
                                                 op0=ALU.mult, op1=ALU.add).then_inc(out_set, 1)
                assert chain[0] == CHAIN, (chain[0], CHAIN)

        @block.tensor
        def _(pe):
            pe.wait_ge(id_set, 1)
            pe.wait_ge(raw_in, 16 * RAWS)
            for bank, raw in enumerate((wq_raw, wv_raw)):
                for oc in range(KC):
                    for hc in range(KC):
                        ins = pe.transpose(ps[:, bank, hc * D + oc * P:hc * D + (oc + 1) * P], raw[:, oc, hc * P:(hc + 1) * P],
                                           ident[:, :])
                ins.then_inc(wt_mm, 1)
            pe.wait_ge(w_set, SPLITS)
            with pe.Fori(0, B, 1) as b:
                def transposes(n):
                    for tb in range(TB):
                        for kc in range(KC):
                            for i in range(4):
                                t = 4 * tb + i
                                if kc == 0:
                                    pe.wait_ge(xn_set, b * 2 * TT + n * TT + t + 1)
                                ins = pe.transpose(ps[:, 2 + KC * tb + kc, i * P:(i + 1) * P], xn[:, t, kc * P:(kc + 1) * P],
                                                   ident[:, :])
                            ins.then_inc(xt_mm, 1)

                def product(dst, pairs):
                    for i, (w, a) in enumerate(pairs):
                        ins = pe.matmul(dst, w, a, start=(i == 0), stop=(i == len(pairs) - 1))
                    return ins

                def three(hi_a, lo_a, hi_b, lo_b):
                    return [(hi_a, hi_b), (hi_a, lo_b), (lo_a, hi_b)]

                transposes(0)
                for u in range(2 * KC * TB):
                    kc, tb = u // TB % KC, u % TB
                    cols = slice(tb * BANK, (tb + 1) * BANK)
                    mc = slice(kc * P, (kc + 1) * P)
                    if u == KC * TB:
                        pe.wait_ge(an_set, 2)
                    if u < TB:
                        pe.wait_ge(xt_l, b * 2 * KC * TB + KC * (tb + 1))
                    if u >= 4:
                        pe.wait_ge(q_l, b * 2 * KC * TB + (KC * TB if u == KC * TB else u - 3))
                    w_h, w_l, a_h, a_l = (wqt_hi, wqt_lo, xt_hi, xt_lo) if u < KC * TB else (an_hi, an_lo, qt_hi, qt_lo)
                    product(ps[:, PB[u % 4], :], [z for c in range(KC) for z in three(w_h[:, c, mc], w_l[:, c, mc], a_h[:, c, cols],
                                                                                      a_l[:, c, cols])]).then_inc(q_mm, 1)
                def v_products():
                    for t in range(TT):
                        rows = slice(t * P, (t + 1) * P)
                        if t >= 4:
                            pe.wait_ge(v_set, b * TT + t - 3)
                        product(ps[:, 2 + t % 4, 0:D], [z for c in range(KC) for z in three(xt_hi[:, c, rows], xt_lo[:, c, rows],
                                                                                            wvt_hi[:, c, :], wvt_lo[:, c, :])]).then_inc(v_mm, 1)

                pe.wait_ge(q_l, b * 2 * KC * TB + 2 * KC * TB)

                def values(t):
                    if t == 0:
                        pe.wait_ge(v_parts, b * 2 + 2)
                    pe.wait_ge(pt_l, b * TT + t + 1)
                    if t >= 2:
                        pe.wait_ge(h_set, b * TT + t - 1)
                    product(ps[:, 6 + t % 2, 0:D], [z for c in range(TT) for z in three(
                        pt_hi[:, t % 2, c, :], pt_lo[:, t % 2, c, :], v_hi[:, c, :], v_lo[:, c, :])]).then_inc(pv_mm, 1)

                def turn(t):
                    pe.wait_ge(p_set, b * TT + t + 1)
                    if t >= 2:
                        pe.wait_ge(pt_l, b * TT + t - 1)
                    for c in range(TT):
                        bank = 2 + 2 * (t % 2) + c // 4
                        ins = pe.transpose(ps[:, bank, c % 4 * P:(c % 4 + 1) * P], pr[:, t % 2, c * P:(c + 1) * P], ident[:, :])
                    ins.then_inc(pt_mm, 1)

                for t in range(TT + 2):
                    if t < TT:
                        rows = slice(t * P, (t + 1) * P)
                        if t:
                            pe.wait_ge(p_set, b * TT + t)
                        for kh in range(2):
                            keys = slice(kh * BANK, (kh + 1) * BANK)
                            ins = product(ps[:, kh, :], [z for c in range(KC) for z in three(
                                qt_hi[:, c, rows], qt_lo[:, c, rows], tq_hi[:, c, keys], tq_lo[:, c, keys])])
                        ins.then_inc(s_mm, 1)
                    if t == 0:
                        v_products()
                    if t == 1:
                        pe.wait_ge(v_set, b * TT + TT)
                    if 1 <= t <= TT:
                        turn(t - 1)
                    if t >= 2:
                        values(t - 2)
                transposes(1)
                pe.wait_ge(f_lo, SPLITS2)
                pe.wait_ge(c_in, 16 * CONSTS)
                for u in range(TB * MH):
                    tb, m = u // MH, u % MH
                    cols = slice(tb * BANK, (tb + 1) * BANK)
                    mc = slice(m * P, (m + 1) * P)
                    if m == 0:
                        pe.wait_ge(xt_l, b * 2 * KC * TB + KC * TB + KC * (tb + 1))
                    if u >= 4:
                        pe.wait_ge(f_set, b * FU + u - 3)
                    product(ps[:, PB[u % 4], :], [z for c in range(KC) for z in three(
                        enc_hi[:, c, mc], enc_lo[:, c, mc], xt_hi[:, c, cols], xt_lo[:, c, cols])]).then_inc(f_mm, 1)
                for tb in range(TB):
                    cols = slice(tb * BANK, (tb + 1) * BANK)
                    pe.wait_ge(f_split, b * FU + MH * (tb + 1))
                    product(ps[:, 2 + tb, :], [z for m in range(MH) for z in three(
                        s2c_hi[:, m, :, :].rearrange("p a c -> p (a c)"), s2c_lo[:, m, :, :].rearrange("p a c -> p (a c)"),
                        sp_hi[:, m, cols], sp_lo[:, m, cols])]).then_inc(f_mm, 1)
                for tb in range(TB):
                    cols = slice(tb * BANK, (tb + 1) * BANK)
                    pe.wait_ge(f_split, b * FU + TB * MH + tb + 1)
                    product(ps[:, 4 + tb, :], [(w[:, :, :].rearrange("p a c -> p (a c)"), cs[:, cols])
                                               for w in (rw1_hi, rw1_lo)]).then_inc(f_mm, 1)
                for t in range(TT):
                    if t % 4 == 0:
                        pe.wait_ge(f_split, b * FU + TB * MH + TB + t // 4 + 1)
                    ins = product(ps[:, 2, t * E:(t + 1) * E], [(rs[:, t * P:(t + 1) * P], w[:, :]) for w in (rw2_hi, rw2_lo)])
                ins.then_inc(lg_mm, 1)

                def experts_in(v):
                    for n in range(4 * v, 4 * v + 4):
                        tb, e, hh = n // (E * EH), n // EH % E, n % EH
                        if n >= 2:
                            pe.wait_ge(eh_set, b * TB * E * EH + n - 1)
                        product(ps[:, n % 2, :], [(w[:, e, hh * P:(hh + 1) * P], cs[:, tb * BANK:(tb + 1) * BANK])
                                                  for w in (ew1_hi, ew1_lo)]).then_inc(e1_mm, 1)

                def gates(v):
                    tb, q = v // PAIRS, v % PAIRS
                    if v >= 2:
                        pe.wait_ge(cb_set, b * TB * PAIRS + v - 1)
                    pe.wait_ge(gate_set, b * TB * PAIRS + v + 1)
                    for i in range(4):
                        ins = pe.transpose(ps[:, 4 + v % 2, i * P:(i + 1) * P],
                                           gate_w[:, 4 * tb + i, 2 * q:2 * q + 2, :].rearrange("p a c -> p (a c)"), ident[:, :])
                    ins.then_inc(cb_mm, 1)

                def experts_out(v):
                    q = v % PAIRS
                    pe.wait_ge(eh_set, b * TB * E * EH + 4 * v + 4)
                    if v >= 2:
                        pe.wait_ge(y_set, b * TB * PAIRS + v - 1)
                    for hh in range(EH):
                        for i in range(2):
                            ins = pe.matmul(ps[C * i:C * i + C, 6 + v % 2, :], ew2_sb[:, 2 * q + i, hh, :],
                                            eh[:, (4 * v + 2 * i + hh) % 8, :], start=(hh == 0), stop=(hh == EH - 1))
                    ins.then_inc(e2_mm, 1)

                experts_in(0)
                experts_in(1)
                for v in range(TB * PAIRS):
                    gates(v)
                    experts_out(v)
                    if v + 2 < TB * PAIRS:
                        experts_in(v + 2)
                for u in range(TB * MH):
                    tb, m = u // MH, u % MH
                    cols = slice(tb * BANK, (tb + 1) * BANK)
                    mc = slice(m * P, (m + 1) * P)
                    if m == 0:
                        pe.wait_ge(ys_set, b * TB + tb + 1)
                    if u == 0:
                        pe.wait_ge(y_set, b * TB * PAIRS + TB * PAIRS)
                    if u >= 4:
                        pe.wait_ge(f_set, b * FU + TB * MH + 2 * TB + u - 3)
                    product(ps[:, PB[u % 4], :], three(c2s_hi[:, mc], c2s_lo[:, mc], ys_hi[:, cols], ys_lo[:, cols])).then_inc(f_mm, 1)
                for t in range(TT):
                    rows = slice(t * P, (t + 1) * P)
                    if t % 4 == 0:
                        pe.wait_ge(f_split, b * FU + TB * MH + 2 * TB + MH * (t // 4 + 1))
                    if t >= 4:
                        pe.wait_ge(de_set, b * TT + t - 3)
                    product(ps[:, 2 + t % 4, 0:D], [z for m in range(MH) for z in three(
                        rt_hi[:, m, rows], rt_lo[:, m, rows], dec_hi[:, m, :], dec_lo[:, m, :])]).then_inc(de_mm, 1)

def two_layers(nc, x, tok_w, *rest):
    layer0, layer1, out = rest[:8], rest[8:-1], rest[-1]
    wq, wv, anomaly = layer1[0], layer1[2], layer1[4]
    early = [nc.alloc_sbuf_tensor_at(f"{name}_raw", [P, w.shape[0] // P, w.shape[1]], F32,
                                     offset=EARLY_AT + i * 4 * w.shape[0] // P * w.shape[1])
             for i, (name, w) in enumerate((("wq", wq), ("wv", wv), ("an", anomaly)))]
    loads = [(t[:, :, :], w.rearrange("(k p) n -> p k n", p=P)) for t, w in zip(early, (wq, wv, anomaly))]
    h_mid = nc.dram_tensor("h_mid", [x.shape[0], x.shape[1], tok_w.shape[1]], F32, kind="Internal").ap()
    with nc.semaphore("early_in") as early_in:
        first_layer(nc, x, tok_w, *layer0, h_mid, loads, early_in)
        second_layer(nc, h_mid, *layer1, out, early, early_in)


_INS = [
    'x', 'L0_tok_W', 'L0_attn_qkv_w', 'L0_attn_qkv_b', 'L0_attn_proj_w', 'L0_attn_proj_b', 'L0_ffn_w1',
    'L0_ffn_b1', 'L0_ffn_w2', 'L0_ffn_b2', 'L1_attn_Wq', 'L1_attn_bq', 'L1_attn_Wv', 'L1_attn_bv',
    'L1_attn_anomaly_matrix', 'L1_ffn_enc_w', 'L1_ffn_enc_b', 'L1_ffn_s2c_w', 'L1_ffn_s2c_b', 'L1_ffn_r_w1',
    'L1_ffn_r_b1', 'L1_ffn_r_w2', 'L1_ffn_r_b2', 'L1_ffn_e_w1', 'L1_ffn_e_b1', 'L1_ffn_e_w2', 'L1_ffn_e_b2',
    'L1_ffn_c2s_w', 'L1_ffn_c2s_b', 'L1_ffn_dec_w', 'L1_ffn_dec_b', 'L1_ffn_ln_g', 'L1_ffn_ln_b',
]


def kernel(**inputs):
    import numpy as _np
    import concourse.bacc as _bacc
    from concourse import mybir as _mybir
    from concourse.bass_utils import run_bass_kernel_spmd as _run

    nc = _bacc.Bacc("TRN2", target_bir_lowering=False, num_devices=1)
    arrays, args = {}, []
    for name in _INS:
        a = _np.ascontiguousarray(inputs[name])
        arrays[f"in_{name}_dram"] = a
        args.append(nc.dram_tensor(f"in_{name}_dram", a.shape, _mybir.dt.from_np(a.dtype), kind="ExternalInput").ap())
    shape = [*inputs["x"].shape, inputs["L0_tok_W"].shape[1]]
    args.append(nc.dram_tensor("out_dram", shape, _mybir.dt.float32, kind="ExternalOutput").ap())
    two_layers(nc, *args)
    r = _run(nc, [arrays], core_ids=[0])
    return r.results[0]["out_dram"]
```
